# Optimizing a Trainium2 kernel written in Bass

```python
import numpy as np
import jax
import jax.numpy as jnp

def _softmax(x, axis=-1):
    return jax.nn.softmax(x, axis=axis)

def _gelu(x):
    return jax.nn.gelu(x, approximate=True)

def _silu(x):
    return jax.nn.silu(x)

def _sigmoid(x):
    return jax.nn.sigmoid(x)

def _layernorm(x, axis=-1, eps=1e-05):
    m = jnp.mean(x, axis=axis, keepdims=True)
    v = jnp.var(x, axis=axis, keepdims=True)
    return (x - m) / jnp.sqrt(v + eps)

def _scatter_add(tgt, idx, src, axis=0):
    return tgt.at[idx].add(src)

def _segment_sum(src, seg, n):
    return jax.ops.segment_sum(src, seg, n)
kernel_name = 'mk_dlrm_tower_d1_rec_r8_0c508f'

def setup_inputs(seed: int=0):
    np.random.seed(seed)
    _w = jnp.asarray

    def _rec_inputs():
        import jax
        import jax.numpy as jnp
        _tk = jax.random.key(seed)
        ids = jnp.stack([jax.random.randint(jax.random.fold_in(_tk, 200 + f), (2048,), 0, v, jnp.int32) for f, v in enumerate([12500, 12500, 1250, 1000, 125000, 1000, 1000, 1000, 1250, 1250, 12500, 12500, 12500, 1250, 12500, 1250, 1250, 1000, 1000, 1250, 1250, 1000, 12500, 1000, 12500, 1250])], axis=1)
        tbl_0 = 0.05 * jax.random.normal(jax.random.fold_in(_tk, 500 + 0), (12500, 128), jnp.float32)
        tbl_1 = 0.05 * jax.random.normal(jax.random.fold_in(_tk, 500 + 1), (12500, 128), jnp.float32)
        tbl_2 = 0.05 * jax.random.normal(jax.random.fold_in(_tk, 500 + 2), (1250, 128), jnp.float32)
        tbl_3 = 0.05 * jax.random.normal(jax.random.fold_in(_tk, 500 + 3), (1000, 128), jnp.float32)
        tbl_4 = 0.05 * jax.random.normal(jax.random.fold_in(_tk, 500 + 4), (125000, 128), jnp.float32)
        tbl_5 = 0.05 * jax.random.normal(jax.random.fold_in(_tk, 500 + 5), (1000, 128), jnp.float32)
        tbl_6 = 0.05 * jax.random.normal(jax.random.fold_in(_tk, 500 + 6), (1000, 128), jnp.float32)
        tbl_7 = 0.05 * jax.random.normal(jax.random.fold_in(_tk, 500 + 7), (1000, 128), jnp.float32)
        tbl_8 = 0.05 * jax.random.normal(jax.random.fold_in(_tk, 500 + 8), (1250, 128), jnp.float32)
        tbl_9 = 0.05 * jax.random.normal(jax.random.fold_in(_tk, 500 + 9), (1250, 128), jnp.float32)
        tbl_10 = 0.05 * jax.random.normal(jax.random.fold_in(_tk, 500 + 10), (12500, 128), jnp.float32)
        tbl_11 = 0.05 * jax.random.normal(jax.random.fold_in(_tk, 500 + 11), (12500, 128), jnp.float32)
        tbl_12 = 0.05 * jax.random.normal(jax.random.fold_in(_tk, 500 + 12), (12500, 128), jnp.float32)
        tbl_13 = 0.05 * jax.random.normal(jax.random.fold_in(_tk, 500 + 13), (1250, 128), jnp.float32)
        tbl_14 = 0.05 * jax.random.normal(jax.random.fold_in(_tk, 500 + 14), (12500, 128), jnp.float32)
        tbl_15 = 0.05 * jax.random.normal(jax.random.fold_in(_tk, 500 + 15), (1250, 128), jnp.float32)
        tbl_16 = 0.05 * jax.random.normal(jax.random.fold_in(_tk, 500 + 16), (1250, 128), jnp.float32)
        tbl_17 = 0.05 * jax.random.normal(jax.random.fold_in(_tk, 500 + 17), (1000, 128), jnp.float32)
        tbl_18 = 0.05 * jax.random.normal(jax.random.fold_in(_tk, 500 + 18), (1000, 128), jnp.float32)
        tbl_19 = 0.05 * jax.random.normal(jax.random.fold_in(_tk, 500 + 19), (1250, 128), jnp.float32)
        tbl_20 = 0.05 * jax.random.normal(jax.random.fold_in(_tk, 500 + 20), (1250, 128), jnp.float32)
        tbl_21 = 0.05 * jax.random.normal(jax.random.fold_in(_tk, 500 + 21), (1000, 128), jnp.float32)
        tbl_22 = 0.05 * jax.random.normal(jax.random.fold_in(_tk, 500 + 22), (12500, 128), jnp.float32)
        tbl_23 = 0.05 * jax.random.normal(jax.random.fold_in(_tk, 500 + 23), (1000, 128), jnp.float32)
        tbl_24 = 0.05 * jax.random.normal(jax.random.fold_in(_tk, 500 + 24), (12500, 128), jnp.float32)
        tbl_25 = 0.05 * jax.random.normal(jax.random.fold_in(_tk, 500 + 25), (1250, 128), jnp.float32)
        _rk = jax.random.fold_in(_tk, 7)
        r_dense_features = -0.000520686 + 1.00062 * jax.random.normal(jax.random.fold_in(_rk, 101), (2048, 128), jnp.float32)
        W_top1 = 0.0405887 * jax.random.normal(jax.random.fold_in(_tk, 801), (607, 512), jnp.float32)
        W_top2 = 0.0441942 * jax.random.normal(jax.random.fold_in(_tk, 802), (512, 256), jnp.float32)
        W_top3 = 0.0625 * jax.random.normal(jax.random.fold_in(_tk, 803), (256, 1), jnp.float32)
        b_top1 = jnp.zeros((512,), jnp.float32)
        b_top2 = jnp.zeros((256,), jnp.float32)
        return (r_dense_features, ids, tbl_0, tbl_1, tbl_2, tbl_3, tbl_4, tbl_5, tbl_6, tbl_7, tbl_8, tbl_9, tbl_10, tbl_11, tbl_12, tbl_13, tbl_14, tbl_15, tbl_16, tbl_17, tbl_18, tbl_19, tbl_20, tbl_21, tbl_22, tbl_23, tbl_24, tbl_25, W_top1, b_top1, W_top2, b_top2, W_top3)
    r_dense_features, ids, tbl_0, tbl_1, tbl_2, tbl_3, tbl_4, tbl_5, tbl_6, tbl_7, tbl_8, tbl_9, tbl_10, tbl_11, tbl_12, tbl_13, tbl_14, tbl_15, tbl_16, tbl_17, tbl_18, tbl_19, tbl_20, tbl_21, tbl_22, tbl_23, tbl_24, tbl_25, W_top1, b_top1, W_top2, b_top2, W_top3 = _rec_inputs()

    def _L0_rec_setup():
        import jax, jax.numpy as jnp
        import numpy as np
        F = 26
        N = F + 1
        _TRIU_I, _TRIU_J = np.triu_indices(N, k=1)
        key = jax.random.key(seed)
        k1, k2 = jax.random.split(key)
        B, D = (2048, 128)
        dense_features = jax.random.normal(k1, (B, D), dtype=jnp.float32)
        sparse_features = jax.random.normal(k2, (B, F, D), dtype=jnp.float32)
        return {'dense_features': dense_features, 'sparse_features': sparse_features}
    _L0_rec_all = _L0_rec_setup()
    _L0_rec_in = {k: v for k, v in _L0_rec_all.items() if k in ()}
    del _L0_rec_all
    return {'r_dense_features': r_dense_features, 'ids': ids, 'tbl_0': tbl_0, 'tbl_1': tbl_1, 'tbl_2': tbl_2, 'tbl_3': tbl_3, 'tbl_4': tbl_4, 'tbl_5': tbl_5, 'tbl_6': tbl_6, 'tbl_7': tbl_7, 'tbl_8': tbl_8, 'tbl_9': tbl_9, 'tbl_10': tbl_10, 'tbl_11': tbl_11, 'tbl_12': tbl_12, 'tbl_13': tbl_13, 'tbl_14': tbl_14, 'tbl_15': tbl_15, 'tbl_16': tbl_16, 'tbl_17': tbl_17, 'tbl_18': tbl_18, 'tbl_19': tbl_19, 'tbl_20': tbl_20, 'tbl_21': tbl_21, 'tbl_22': tbl_22, 'tbl_23': tbl_23, 'tbl_24': tbl_24, 'tbl_25': tbl_25, 'W_top1': W_top1, 'b_top1': b_top1, 'W_top2': W_top2, 'b_top2': b_top2, 'W_top3': W_top3}

def reference(r_dense_features, ids, tbl_0, tbl_1, tbl_2, tbl_3, tbl_4, tbl_5, tbl_6, tbl_7, tbl_8, tbl_9, tbl_10, tbl_11, tbl_12, tbl_13, tbl_14, tbl_15, tbl_16, tbl_17, tbl_18, tbl_19, tbl_20, tbl_21, tbl_22, tbl_23, tbl_24, tbl_25, W_top1, b_top1, W_top2, b_top2, W_top3):
    import jax
    import jax.numpy as jnp

    def _L0_rec_ref(dense_features, sparse_features):
        import jax, jax.numpy as jnp
        import numpy as np
        F = 26
        N = F + 1
        _TRIU_I, _TRIU_J = np.triu_indices(N, k=1)
        combined = jnp.concatenate([dense_features[:, None, :], sparse_features], axis=1)
        interactions = jnp.einsum('bnd,bmd->bnm', combined, combined)
        interactions_flat = interactions[:, _TRIU_I, _TRIU_J]
        return jnp.concatenate([dense_features, interactions_flat], axis=1)
    e = jnp.stack([tbl_0[ids[:, 0]], tbl_1[ids[:, 1]], tbl_2[ids[:, 2]], tbl_3[ids[:, 3]], tbl_4[ids[:, 4]], tbl_5[ids[:, 5]], tbl_6[ids[:, 6]], tbl_7[ids[:, 7]], tbl_8[ids[:, 8]], tbl_9[ids[:, 9]], tbl_10[ids[:, 10]], tbl_11[ids[:, 11]], tbl_12[ids[:, 12]], tbl_13[ids[:, 13]], tbl_14[ids[:, 14]], tbl_15[ids[:, 15]], tbl_16[ids[:, 16]], tbl_17[ids[:, 17]], tbl_18[ids[:, 18]], tbl_19[ids[:, 19]], tbl_20[ids[:, 20]], tbl_21[ids[:, 21]], tbl_22[ids[:, 22]], tbl_23[ids[:, 23]], tbl_24[ids[:, 24]], tbl_25[ids[:, 25]]], axis=1)
    z = _L0_rec_ref(r_dense_features, e)
    z = z.reshape(z.shape[0], -1)
    h = jnp.concatenate([z, r_dense_features], axis=1)
    h = jnp.maximum(h @ W_top1 + b_top1, 0.0)
    h = jnp.maximum(h @ W_top2 + b_top2, 0.0)
    y = h @ W_top3
    return y

_drawn_inputs = setup_inputs


def setup_inputs(seed=0):
    import zlib

    import numpy as np

    out = dict(_drawn_inputs(seed))
    spreads = {'b_top1': (0.0, 0.1), 'b_top2': (0.0, 0.1)}
    factors = {}
    for name, (base, spread) in spreads.items():
        noise = np.random.default_rng([zlib.crc32(name.encode()), seed]).standard_normal(out[name].shape)
        drawn = base * np.exp(spread * noise) if base else spread * noise
        out[name] = jnp.asarray(drawn.astype(out[name].dtype))
    for name, factor in factors.items():
        out[name] = (out[name] * factor).astype(out[name].dtype)
    return out
```

```python
from contextlib import ExitStack

import concourse.bass as bass
import numpy as np
from concourse import mybir

BATCH, FIELDS, D = 2048, 26, 128
VOCABS = [12500, 12500, 1250, 1000, 125000, 1000, 1000, 1000, 1250, 1250, 12500, 12500, 12500,
          1250, 12500, 1250, 1250, 1000, 1000, 1250, 1250, 1000, 12500, 1000, 12500, 1250]
H1, H2 = 512, 256
P = 128

ONEHOT_TABLES = [f for f, v in enumerate(VOCABS) if v == 1000]
GATHER_TABLES = [f for f in range(FIELDS) if f not in ONEHOT_TABLES]
NO, NG = len(ONEHOT_TABLES), len(GATHER_TABLES)
VROWS = 125
CHUNKS = 1000 // VROWS

N = FIELDS + 1
NK = N // 2
SLOT_FEATURE = [1 + f for f in ONEHOT_TABLES] + [0] + [1 + f for f in GATHER_TABLES]
DENSE_SLOT = NO
ROWS_IN = 1 + NG

MC = 256
MACROS = BATCH // MC
TILES = 2
STRIPS = 4
SS = P // STRIPS
BANK_SAMPLES = 16
TR_GROUPS = [(g, min(4, ROWS_IN - g)) for g in range(0, ROWS_IN, 4)]
NTR = len(TR_GROUPS)
TR_ACT = len(TR_GROUPS[0::2])
TR_DVE = len(TR_GROUPS[1::2])
ICH = 9
PCH = ICH * NK
NPCH = N // ICH
WRAP = N + NK
M1, M2 = H1 // P, H2 // P
STAGES = 4


def build(nc, dense, ids_gather, ids_onehot, tables, w_dense, w_pairs, b1, w2, b2, w3, out):
    F32, F32R, I32 = mybir.dt.float32, mybir.dt.float32r, mybir.dt.int32
    ALU = mybir.AluOpType
    ACT = mybir.ActivationFunctionType

    ctx = ExitStack()
    with ctx:
        def sb(name, shape, dt=F32):
            return ctx.enter_context(nc.sbuf_tensor(name, shape, dt))

        def bank(name):
            return ctx.enter_context(nc.psum_tensor(name, [P, 512], F32))

        def sem(name):
            return ctx.enter_context(nc.semaphore(name))

        rows = [sb(f"rows{t}", [P, ROWS_IN, D]) for t in range(TILES)]
        idx = [sb(f"idx{t}", [P, NG], I32) for t in range(TILES)]
        ET = sb("ET", [P, MC, N])
        tab_hi = sb("tab_hi", [P, NO, CHUNKS, D], F32R)
        tab_lo = sb("tab_lo", [P, NO, CHUNKS, D], F32R)
        stage = [sb(f"stage{k}", [P, CHUNKS, D]) for k in range(STAGES)]
        onehot = [sb(f"onehot{k}", [P, CHUNKS, MC], F32R) for k in range(2)]
        ids_b = sb("ids_b", [P, NO, MC], I32)
        row_id = sb("row_id", [P, CHUNKS], I32)
        gram = sb("gram", [P, N, TILES * SS])
        pairs = sb("pairs", [P, NPCH, MC])
        denseT = sb("denseT", [P, MC])
        wd = sb("wd", [P, 2, H1])
        wp = sb("wp", [P, NPCH, H1])
        w2s = sb("w2s", [P, M1, H2])
        w3s = sb("w3s", [P, M2])
        b1s = sb("b1s", [P, M1])
        b2s = sb("b2s", [P, M2])
        h1 = sb("h1", [P, M1, MC])
        h2 = sb("h2", [P, M2, MC])
        y = sb("y", [1, MC])
        ident = sb("ident", [P, P])

        TR = [bank("tr_even"), bank("tr_odd")]
        OH = [bank("oh_a"), bank("oh_b")]
        GR = [bank("gr_a"), bank("gr_b")]
        ML = [bank("mlp_a"), bank("mlp_b")]

        scratch = nc.dram_tensor("gram_scratch", [N * (WRAP + 1), MC], F32, kind="Internal").ap()
        scratch_rows = scratch[0:N * WRAP, :].rearrange("(i j) c -> i j c", j=WRAP)
        scratch_pairs = scratch.rearrange("(i k) c -> i k c", k=WRAP + 1)

        ident_zero, ident_made, row_ids_made = sem("ident_zero"), sem("ident_made"), sem("row_ids_made")
        idx_loaded = [sem(f"idx_loaded{t}") for t in range(TILES)]
        dense_loaded = [sem(f"dense_loaded{t}") for t in range(TILES)]
        gathered = [sem(f"gathered{t}") for t in range(TILES)]
        tiles_begun = sem("tiles_begun")
        ids_loaded = sem("ids_loaded")
        table_loaded = [sem(f"table_loaded{k}") for k in range(STAGES)]
        weights_loaded, wd_summed = sem("weights_loaded"), sem("wd_summed")
        hi_made, lo_made = sem("hi_made"), sem("lo_made")
        gram_cleared = sem("gram_cleared")
        onehot_made = sem("onehot_made")
        looked_up = sem("looked_up")
        lookup_copied = sem("lookup_copied")
        transposed = sem("transposed")
        tr_copied_act, tr_copied_dve = sem("tr_copied_act"), sem("tr_copied_dve")
        gram_done, gram_copied = sem("gram_done"), sem("gram_copied")
        scratch_written = sem("scratch_written")
        pairs_loaded = sem("pairs_loaded")
        denseT_made = sem("denseT_made")
        l1_done, h1_made = sem("l1_done"), sem("h1_made")
        l2_done, h2_made = sem("l2_done"), sem("h2_made")
        y_done, y_copied = sem("y_done"), sem("y_copied")
        y_stored = sem("y_stored")

        block = ctx.enter_context(nc.Block())

        @block.sync
        def _(sp):
            def load_tile(tile, t):
                sp.dma_start(idx[t][:, :], ids_gather[tile, :, :]).then_inc(idx_loaded[t], 16)
                sp.dma_start(rows[t][:, 0, :], dense[tile, :, :]).then_inc(dense_loaded[t], 16)

            def load_ids(m):
                sp.dma_start(ids_b[:, :, :], ids_onehot[m, :, :].partition_broadcast(P)).then_inc(ids_loaded, 16)

            def gram_through_scratch(m):
                sp.wait_ge(gram_copied, 4 * m + 4)
                for g in range(STRIPS):
                    cols = slice(g * TILES * SS, (g + 1) * TILES * SS)
                    sp.dma_start(scratch_rows[:, 0:N, cols], gram[32 * g:32 * g + N, :, :]) \
                      .then_inc(scratch_written, 16)
                    sp.dma_start(scratch_rows[N - NK:N, N:WRAP, cols],
                                 gram[32 * g + N - NK:32 * g + N, 0:NK, :]).then_inc(scratch_written, 16)
                sp.wait_ge(scratch_written, 32 * STRIPS * (m + 1))
                for c in range(NPCH):
                    sp.dma_start(pairs[0:PCH, c, :], scratch_pairs[c * ICH:(c + 1) * ICH, 1:1 + NK, :]) \
                      .then_inc(pairs_loaded, 16)

            def store_y(m):
                sp.wait_ge(y_copied, m + 1)
                sp.dma_start(out[bass.ds(m, 1), :], y[0:1, :]) \
                  .then_inc(y_stored, 16)

            def next_tile(m, t):
                sp.wait_ge(transposed, 2 * NTR * m + NTR * (t + 1))
                load_tile((m + 1) * TILES + t, t)

            for t in range(TILES):
                load_tile(t, t)
            load_ids(0)
            for n in range(NO):
                k = n % STAGES
                if n >= STAGES:
                    sp.wait_ge(hi_made, n - STAGES + 1)
                    sp.wait_ge(lo_made, n - STAGES + 1)
                sp.dma_start(stage[k][0:VROWS, :, :], tables[ONEHOT_TABLES[n]].rearrange("(p q) d -> p q d", q=CHUNKS)) \
                  .then_inc(table_loaded[k], 16)
            for dst, src in ((wd, w_dense), (wp[0:PCH], w_pairs), (w2s, w2), (w3s, w3), (b1s, b1), (b2s, b2)):
                sp.dma_start(dst[:], src).then_inc(weights_loaded, 16)

            sp.wait_ge(onehot_made, NO)
            load_ids(1)
            next_tile(0, 0)
            next_tile(0, 1)
            gram_through_scratch(0)
            with sp.Fori(1, MACROS - 1) as m:
                next_tile(m, 0)
                sp.wait_ge(onehot_made, NO * m + NO)
                load_ids(m + 1)
                store_y(m - 1)
                next_tile(m, 1)
                gram_through_scratch(m)
            store_y(MACROS - 2)
            gram_through_scratch(MACROS - 1)
            store_y(MACROS - 1)
            sp.wait_ge(y_stored, 16 * MACROS)

        @block.gpsimd
        def _(pool):
            pool.memset(ident[:, :], 0.0).then_inc(ident_zero, 1)
            pool.iota(row_id[:, :], [[1, CHUNKS]], 0, CHUNKS).then_inc(row_ids_made, 1)
            pool.wait_ge(ident_zero, 1)
            pool.affine_select(out=ident[:, :], in_=ident[:, :], compare_op=ALU.not_equal, fill=1.0,
                               base=0, pattern=[[-1, P]], channel_multiplier=1).then_inc(ident_made, 1)

            def gather_tile(m, t, first):
                pool.wait_ge(idx_loaded[t], 16 * m + 16)
                if not first:
                    pool.wait_ge(transposed, 2 * NTR * (m - 1) + NTR * (t + 1))
                pool.sem_inc(tiles_begun, 1)
                for n, f in enumerate(GATHER_TABLES):
                    pool.indirect_dma_start(
                        out=rows[t][:, 1 + n, :], out_offset=None, in_=tables[f],
                        in_offset=bass.IndirectOffsetOnAxis(ap=idx[t][:, n:n + 1], axis=0),
                    ).then_inc(gathered[t], 16)

            for t in range(TILES):
                gather_tile(0, t, True)
            with pool.Fori(1, MACROS) as m:
                for t in range(TILES):
                    gather_tile(m, t, False)

        @block.tensor
        def _(pe):
            def transpose_group(m, t, g, first):
                f0, nf = TR_GROUPS[g]
                if g == 0:
                    pe.wait_ge(dense_loaded[t], 16 * m + 16)
                    pe.wait_ge(gathered[t], 16 * NG * m + 16 * NG)
                if g % 2 == 0:
                    n = TR_ACT * t + g // 2
                    if not (first and n == 0):
                        pe.wait_ge(tr_copied_act, 2 * TR_ACT * m + n)
                else:
                    n = TR_DVE * t + g // 2
                    if not (first and n == 0):
                        pe.wait_ge(tr_copied_dve, 2 * TR_DVE * m + n)
                for k in range(nf):
                    last = pe.transpose(TR[g % 2][:, k * P:(k + 1) * P], rows[t][:, f0 + k, :], ident[:, :])
                last.then_inc(transposed, 1)

            def lookup(m, n, first):
                pe.wait_ge(onehot_made, NO * m + n + 1)
                if not (first and n < 2):
                    pe.wait_ge(lookup_copied, NO * m + n - 1)
                if first:
                    pe.wait_ge(hi_made, n + 1)
                    pe.wait_ge(lo_made, n + 1)
                for q in range(CHUNKS):
                    for part in (tab_hi, tab_lo):
                        last = pe.matmul(OH[n % 2][:, 0:MC], part[0:VROWS, n, q, :], onehot[n % 2][0:VROWS, q, :],
                                         start=(q == 0 and part is tab_hi), stop=(q == CHUNKS - 1 and part is tab_lo))
                last.then_inc(looked_up, 1)

            def gram_half(m, t, b, half, first):
                if half == 0:
                    if not (first and t == 0):
                        pe.wait_ge(gram_copied, 4 * m + 2 * t + b - 1)
                    if t == 0 and b == 0:
                        pe.wait_ge(lookup_copied, NO * m + NO)
                    if b == 0:
                        pe.wait_ge(tr_copied_act, 2 * TR_ACT * m + TR_ACT * (t + 1))
                        pe.wait_ge(tr_copied_dve, 2 * TR_DVE * m + TR_DVE * (t + 1))
                    if first and t == 0 and b == 0:
                        pe.wait_ge(gram_cleared, 2)
                hs = BANK_SAMPLES // 2
                for s in range(half * hs, (half + 1) * hs):
                    for g in range(STRIPS):
                        c = g * TILES * SS + t * SS + b * BANK_SAMPLES + s
                        last = pe.matmul(GR[b][32 * g:32 * g + N, s * N:(s + 1) * N], ET[:, c, :], ET[:, c, :],
                                         start=True, stop=True)
                if half == 1:
                    last.then_inc(gram_done, 1)

            def layer1(m, c, first):
                if c == 0:
                    pe.wait_ge(pairs_loaded, 16 * NPCH * m + 16 * NPCH)
                    pe.wait_ge(denseT_made, m + 1)
                    if first:
                        pe.wait_ge(weights_loaded, 16 * 6)
                        pe.wait_ge(wd_summed, 1)
                    else:
                        pe.wait_ge(y_copied, m)
                elif c == 1:
                    if not first:
                        pe.wait_ge(h2_made, M2 * m)
                else:
                    pe.wait_ge(h1_made, M1 * m + c - 1)
                hid = slice(c * P, (c + 1) * P)
                pe.matmul(ML[c % 2][:, 0:MC], wd[:, 0, hid], denseT[:, :], start=True, stop=False)
                for k in range(NPCH):
                    last = pe.matmul(ML[c % 2][:, 0:MC], wp[0:PCH, k, hid], pairs[0:PCH, k, :],
                                     start=False, stop=(k == NPCH - 1))
                last.then_inc(l1_done, 1)

            def layer2(m, c):
                pe.wait_ge(h1_made, M1 * m + M1)
                for k in range(M1):
                    last = pe.matmul(ML[c % 2][:, 0:MC], w2s[:, k, c * P:(c + 1) * P], h1[:, k, :],
                                     start=(k == 0), stop=(k == M1 - 1))
                last.then_inc(l2_done, 1)

            def layer3(m):
                pe.wait_ge(h2_made, M2 * m + M2)
                for k in range(M2):
                    last = pe.matmul(ML[0][0:1, 0:MC], w3s[:, k:k + 1], h2[:, k, :],
                                     start=(k == 0), stop=(k == M2 - 1))
                last.then_inc(y_done, 1)

            def tile1_and_grams(m, first):
                gram_half(m, 0, 0, 0, first)
                gram_half(m, 0, 0, 1, first)
                transpose_group(m, 1, 0, first)
                transpose_group(m, 1, 1, first)
                gram_half(m, 0, 1, 0, first)
                transpose_group(m, 1, 2, first)
                transpose_group(m, 1, 3, first)
                gram_half(m, 0, 1, 1, first)
                for g in range(4, NTR):
                    transpose_group(m, 1, g, first)
                for b in range(2):
                    for half in range(2):
                        gram_half(m, 1, b, half, first)

            for n in range(NO):
                lookup(0, n, True)
            pe.wait_ge(ident_made, 1)
            for g in range(NTR):
                transpose_group(0, 0, g, True)
            tile1_and_grams(0, True)

            def macro(m, mlp_first):
                transpose_group(m, 0, 0, False)
                transpose_group(m, 0, 1, False)
                lookup(m, 0, False)
                transpose_group(m, 0, 2, False)
                transpose_group(m, 0, 3, False)
                lookup(m, 1, False)
                for g in range(4, NTR):
                    transpose_group(m, 0, g, False)
                lookup(m, 2, False)
                lookup(m, 3, False)
                layer1(m - 1, 0, mlp_first)
                lookup(m, 4, False)
                layer1(m - 1, 1, mlp_first)
                layer1(m - 1, 2, mlp_first)
                lookup(m, 5, False)
                layer1(m - 1, 3, mlp_first)
                lookup(m, 6, False)
                layer2(m - 1, 0)
                layer2(m - 1, 1)
                lookup(m, 7, False)
                layer3(m - 1)
                tile1_and_grams(m, False)

            macro(1, True)
            with pe.Fori(2, MACROS) as m:
                macro(m, False)
            for c in range(M1):
                layer1(MACROS - 1, c, False)
            for c in range(M2):
                layer2(MACROS - 1, c)
            layer3(MACROS - 1)

        def et_tile(t, f0, nf):
            return ET[:, :, f0:f0 + nf].rearrange("p (g u s) f -> p u f g s", g=STRIPS, u=TILES)[:, t]

        def copy_group(copy, t, g):
            f0, nf = TR_GROUPS[g]
            return copy(et_tile(t, DENSE_SLOT + f0, nf),
                        TR[g % 2][:, 0:nf * P].rearrange("p (f g s) -> p f g s", g=STRIPS, s=SS))

        @block.scalar
        def _(act):
            def copy_lookup(m, n):
                act.wait_ge(looked_up, NO * m + n + 1)
                act.copy(ET[:, :, n], OH[n % 2][:, 0:MC]).then_inc(lookup_copied, 1)

            def copy_transposed(m, t, g, first=False):
                if t == 0 and g == 0 and not first:
                    act.wait_ge(denseT_made, m)
                act.wait_ge(transposed, 2 * NTR * m + NTR * t + g + 1)
                copy_group(act.copy, t, g).then_inc(tr_copied_act, 1)

            def make_h1(m, c):
                act.wait_ge(l1_done, M1 * m + c + 1)
                act.activation(h1[:, c, :], ML[c % 2][:, 0:MC], ACT.Relu, bias=b1s[:, c:c + 1]).then_inc(h1_made, 1)

            def make_h2(m, c):
                act.wait_ge(l2_done, M2 * m + c + 1)
                act.activation(h2[:, c, :], ML[c % 2][:, 0:MC], ACT.Relu, bias=b2s[:, c:c + 1]).then_inc(h2_made, 1)

            def copy_y(m, first):
                act.wait_ge(y_done, m + 1)
                if not first:
                    act.wait_ge(y_stored, 16 * m)
                act.copy(y[0:1, :], ML[0][0:1, 0:MC]).then_inc(y_copied, 1)

            def make_denseT(m):
                act.wait_ge(tr_copied_act, 2 * TR_ACT * m + 2 * TR_ACT)
                act.copy(denseT[:, :], ET[:, :, DENSE_SLOT]).then_inc(denseT_made, 1)

            for n in range(NO):
                act.wait_ge(table_loaded[n % STAGES], 16 * (n // STAGES + 1))
                act.copy(tab_hi[0:VROWS, n, :, :], stage[n % STAGES][0:VROWS, :, :]).then_inc(hi_made, 1)
                if n >= 2:
                    copy_lookup(0, n - 2)
            copy_lookup(0, NO - 2)
            copy_lookup(0, NO - 1)
            for g in range(0, NTR, 2):
                copy_transposed(0, 0, g, True)
            for g in range(0, NTR, 2):
                copy_transposed(0, 1, g)
            make_denseT(0)

            def macro(m, mlp_first):
                copy_transposed(m, 0, 0)
                copy_lookup(m, 0)
                copy_transposed(m, 0, 2)
                copy_lookup(m, 1)
                for g in range(4, NTR, 2):
                    copy_transposed(m, 0, g)
                copy_lookup(m, 2)
                copy_lookup(m, 3)
                make_h1(m - 1, 0)
                copy_lookup(m, 4)
                make_h1(m - 1, 1)
                make_h1(m - 1, 2)
                copy_lookup(m, 5)
                make_h1(m - 1, 3)
                copy_lookup(m, 6)
                make_h2(m - 1, 0)
                make_h2(m - 1, 1)
                copy_lookup(m, 7)
                copy_y(m - 1, mlp_first)
                for g in range(0, NTR, 2):
                    copy_transposed(m, 1, g)
                make_denseT(m)

            macro(1, True)
            with act.Fori(2, MACROS) as m:
                macro(m, False)
            for c in range(M1):
                make_h1(MACROS - 1, c)
            for c in range(M2):
                make_h2(MACROS - 1, c)
            copy_y(MACROS - 1, False)

        @block.vector
        def _(dve):
            def make_onehot(m, n, first):
                if n == 0:
                    dve.wait_ge(ids_loaded, 16 * m + 16)
                if not (first and n < 2):
                    dve.wait_ge(looked_up, NO * m + n - 1)
                dve.tensor_tensor(
                    onehot[n % 2][0:VROWS, :, :],
                    ids_b[0:VROWS, n, :].unsqueeze(1).to_broadcast([VROWS, CHUNKS, MC]),
                    row_id[0:VROWS, :].unsqueeze(2).to_broadcast([VROWS, CHUNKS, MC]),
                    ALU.is_equal).then_inc(onehot_made, 1)

            def copy_transposed(m, t, g):
                dve.wait_ge(transposed, 2 * NTR * m + NTR * t + g + 1)
                copy_group(dve.tensor_copy, t, g).then_inc(tr_copied_dve, 1)

            def copy_gram(m, t, b, first):
                dve.wait_ge(gram_done, 4 * m + 2 * t + b + 1)
                if t == 0 and b == 0 and not first:
                    dve.wait_ge(scratch_written, 32 * STRIPS * m)
                s0 = t * SS + b * BANK_SAMPLES
                dve.tensor_copy(gram[:, :, s0:s0 + BANK_SAMPLES],
                                GR[b][:, 0:BANK_SAMPLES * N].rearrange("p (s j) -> p j s", j=N)) \
                   .then_inc(gram_copied, 1)

            for b in range(2):
                dve.memset(GR[b][:, :], 0.0).then_inc(gram_cleared, 1)
            dve.wait_ge(row_ids_made, 1)
            make_onehot(0, 0, True)
            make_onehot(0, 1, True)
            for n in range(NO):
                dve.wait_ge(hi_made, n + 1)
                dve.tensor_tensor(tab_lo[0:VROWS, n, :, :], stage[n % STAGES][0:VROWS, :, :],
                                  tab_hi[0:VROWS, n, :, :].bitcast(F32), ALU.subtract).then_inc(lo_made, 1)
                if n + 2 < NO:
                    if n >= 0:
                        make_onehot(0, n + 2, True)
            for g in range(1, NTR, 2):
                copy_transposed(0, 0, g)
            dve.wait_ge(weights_loaded, 16 * 6)
            dve.tensor_tensor(wd[:, 0, :], wd[:, 0, :], wd[:, 1, :], ALU.add).then_inc(wd_summed, 1)

            def tile1_and_grams(m, first, last):
                copy_gram(m, 0, 0, first)
                copy_transposed(m, 1, 1)
                copy_transposed(m, 1, 3)
                if not last:
                    make_onehot(m + 1, 0, False)
                copy_gram(m, 0, 1, first)
                if not last:
                    make_onehot(m + 1, 1, False)
                copy_gram(m, 1, 0, first)
                copy_gram(m, 1, 1, first)

            def macro(m, last):
                copy_transposed(m, 0, 1)
                make_onehot(m, 2, False)
                copy_transposed(m, 0, 3)
                for n in range(3, NO):
                    make_onehot(m, n, False)
                tile1_and_grams(m, False, last)

            tile1_and_grams(0, True, False)
            with dve.Fori(1, MACROS - 1) as m:
                macro(m, False)
            macro(MACROS - 1, True)


def _pair_rows():
    found = []
    for i in range(N):
        for k in range(1, NK + 1):
            a, b = sorted((SLOT_FEATURE[i], SLOT_FEATURE[(i + k) % N]))
            found.append(D + a * N - a * (a + 1) // 2 + b - a - 1)
    return np.array(found)


def kernel(**inputs):
    import concourse.bacc as bacc
    from concourse.bass_utils import run_bass_kernel_spmd

    def tiled(a):
        a = a.reshape(MACROS, STRIPS, TILES, SS, a.shape[1]).transpose(0, 2, 1, 3, 4)
        return a.reshape(MACROS * TILES, P, a.shape[-1])

    ids = np.asarray(inputs["ids"])
    w_top1 = np.asarray(inputs["W_top1"])
    ends = w_top1.shape[0] - D
    arrays = {
        "dense": tiled(np.asarray(inputs["r_dense_features"])),
        "ids_gather": tiled(ids[:, GATHER_TABLES]),
        "ids_onehot": ids[:, ONEHOT_TABLES].reshape(MACROS, MC, NO).transpose(0, 2, 1),
        "w_dense": np.stack([w_top1[0:D], w_top1[ends:ends + D]], axis=1),
        "w_pairs": w_top1[_pair_rows()].reshape(NPCH, PCH, H1).transpose(1, 0, 2),
        "b1": np.asarray(inputs["b_top1"]).reshape(M1, P).T,
        "w2": np.asarray(inputs["W_top2"]).reshape(M1, P, H2).transpose(1, 0, 2),
        "b2": np.asarray(inputs["b_top2"]).reshape(M2, P).T,
        "w3": np.asarray(inputs["W_top3"]).reshape(M2, P).T,
    }
    for f in range(FIELDS):
        arrays[f"tbl_{f}"] = np.asarray(inputs[f"tbl_{f}"])
    arrays = {name: np.ascontiguousarray(a) for name, a in arrays.items()}

    nc = bacc.Bacc("TRN2", target_bir_lowering=False, num_devices=1)
    aps = {name: nc.dram_tensor(name, a.shape, mybir.dt.from_np(a.dtype), kind="ExternalInput").ap()
           for name, a in arrays.items()}
    out = nc.dram_tensor("out", (MACROS, MC), mybir.dt.float32, kind="ExternalOutput").ap()
    build(nc, aps["dense"], aps["ids_gather"], aps["ids_onehot"], [aps[f"tbl_{f}"] for f in range(FIELDS)],
          aps["w_dense"], aps["w_pairs"], aps["b1"], aps["w2"], aps["b2"], aps["w3"], out)
    r = run_bass_kernel_spmd(nc, [arrays], core_ids=[0])
    return r.results[0]["out"].reshape(BATCH, 1)
```

```python
from contextlib import ExitStack

import concourse.bass as bass
import numpy as np
from concourse import mybir

BATCH, FIELDS, D = 2048, 26, 128
VOCABS = [12500, 12500, 1250, 1000, 125000, 1000, 1000, 1000, 1250, 1250, 12500, 12500, 12500,
          1250, 12500, 1250, 1250, 1000, 1000, 1250, 1250, 1000, 12500, 1000, 12500, 1250]
H1, H2 = 512, 256
P = 128

NLARGE = 0
WARM = 64
ONEHOTS = 4
ONEHOT_TABLES = [f for f, v in enumerate(VOCABS) if v == 1000] + [f for f, v in enumerate(VOCABS) if v == 1250][:NLARGE]
GATHER_TABLES = [f for f in range(FIELDS) if f not in ONEHOT_TABLES]
NO, NG = len(ONEHOT_TABLES), len(GATHER_TABLES)
VROWS = 125
CHUNKS = [VOCABS[f] // VROWS for f in ONEHOT_TABLES]
CHUNK0 = [sum(CHUNKS[:n]) for n in range(NO + 1)]
MAXCH = max(CHUNKS)

N = FIELDS + 1
NK = N // 2
SLOT_FEATURE = [1 + f for f in ONEHOT_TABLES] + [0] + [1 + f for f in GATHER_TABLES]
DENSE_SLOT = NO
ROWS_IN = 1 + NG

MC = 256
MACROS = BATCH // MC
TILES = 2
STRIPS = 4
SS = P // STRIPS
BANK_SAMPLES = 16
TR_GROUPS = [(g, min(4, ROWS_IN - g)) for g in range(0, ROWS_IN, 4)]
NTR = len(TR_GROUPS)
TR_ACT = len(TR_GROUPS[0::2])
TR_DVE = len(TR_GROUPS[1::2])
GATHERS = [nf - (f0 == 0) for f0, nf in TR_GROUPS]
ICH = 9
PCH = ICH * NK
NPCH = N // ICH
WRAP = N + NK
M1, M2 = H1 // P, H2 // P
LAST = MACROS - 1
STAGES = 3
STAGE = 1024
TABLE_JOBS = [(n, q, min(CHUNKS[n] - q, 8 if CHUNKS[n] <= 8 else 5))
              for n in range(NO) for q in range(0, CHUNKS[n], 8 if CHUNKS[n] <= 8 else 5)]
JOBS_AFTER = [sum(j[0] <= n for j in TABLE_JOBS) for n in range(NO)]
NTJ = len(TABLE_JOBS)


def build(nc, dense, ids_gather, ids_onehot, tables, w_dense, w_pairs, b1, w2, b2, w3, out):
    F32, F32R, I32 = mybir.dt.float32, mybir.dt.float32r, mybir.dt.int32
    ALU = mybir.AluOpType
    ACT = mybir.ActivationFunctionType

    ctx = ExitStack()
    with ctx:
        def sb(name, shape, dt=F32):
            return ctx.enter_context(nc.sbuf_tensor(name, shape, dt))

        def bank(name):
            return ctx.enter_context(nc.psum_tensor(name, [P, 512], F32))

        def sem(name):
            return ctx.enter_context(nc.semaphore(name))

        rows = [sb(f"rows{t}", [P, ROWS_IN, D]) for t in range(TILES)]
        idx = [sb(f"idx{t}", [P, NG], I32) for t in range(TILES)]
        ET = sb("ET", [P, MC, N])
        tab_hi = sb("tab_hi", [P, CHUNK0[NO] * D], F32R)
        tab_lo = sb("tab_lo", [P, CHUNK0[NO] * D], F32R)
        onehot = [sb(f"onehot{k}", [P, MAXCH, MC], F32R) for k in range(ONEHOTS)]
        ids_b = sb("ids_b", [P, NO, MC], I32)
        row_id = {ch: sb(f"row_id{ch}", [P, ch], I32) for ch in sorted(set(CHUNKS))}
        early = sb("early", [P, STAGES * STAGE])
        stage = [early[:, k * STAGE:(k + 1) * STAGE] for k in range(STAGES)]
        GRAM, PAIRS = N * TILES * SS, NPCH * MC
        gram = early[:, 0:GRAM].rearrange("p (j c) -> p j c", j=N)
        pairs = early[:, GRAM:GRAM + PAIRS].rearrange("p (k c) -> p k c", k=NPCH)
        pairs_of_tile = [early[:, GRAM + t * NPCH * P:GRAM + (t + 1) * NPCH * P].rearrange("p (k c) -> p k c", k=NPCH)
                         for t in range(TILES)]
        h1f = [early[:, GRAM + PAIRS + k * MC:GRAM + PAIRS + (k + 1) * MC] for k in range(2)]
        pairs_hi = sb("pairs_hi", [P, NPCH, MC], F32R)
        pairs_lo = sb("pairs_lo", [P, NPCH, MC], F32R)
        denseT_hi = sb("denseT_hi", [P, MC], F32R)
        denseT_lo = sb("denseT_lo", [P, MC], F32R)
        wd_hi, wd_lo = sb("wd_hi", [P, H1], F32R), sb("wd_lo", [P, H1], F32R)
        wp_hi, wp_lo = sb("wp_hi", [P, NPCH * H1], F32R), sb("wp_lo", [P, NPCH * H1], F32R)
        w2_hi, w2_lo = sb("w2_hi", [P, M1 * H2], F32R), sb("w2_lo", [P, M1 * H2], F32R)
        w3s = sb("w3s", [P, M2])
        b1s = sb("b1s", [P, M1])
        b2s = sb("b2s", [P, M2])
        h1_hi = sb("h1_hi", [P, M1, MC], F32R)
        h1_lo = sb("h1_lo", [P, M1, MC], F32R)
        h2 = sb("h2", [P, M2, TILES, P])
        y = sb("y", [P, MC // P])
        ident = sb("ident", [P, P])

        TR = [bank("tr_even"), bank("tr_odd")]
        OH = [bank("oh_a"), bank("oh_b")]
        GR = [bank("gr_a"), bank("gr_b")]
        ML = [bank("mlp_a"), bank("mlp_b")]

        scratch = nc.dram_tensor("scratch", [32 * (WRAP + 1), MC], F32, kind="Internal").ap()
        scratch_of_tile = [nc.dram_tensor(f"scratch_of_tile{t}", [32 * (WRAP + 1), P], F32, kind="Internal").ap()
                           for t in range(TILES)]

        def scratch_main(scr, cols):
            return scr[0:32 * WRAP, cols].rearrange("(i j) c -> i j c", j=WRAP)[:, 0:N, :]

        def scratch_wrap(scr, cols):
            return scr[0:32 * WRAP, cols].rearrange("(i j) c -> i j c", j=WRAP)[N - NK:N, N:WRAP, :]

        def scratch_pairs(scr, k):
            return scr.rearrange("(i k) c -> i k c", k=WRAP + 1)[k * ICH:(k + 1) * ICH, 1:1 + NK, :]


        def tile_cols(ap, t):
            lead = " ".join("abcd"[:len(ap.shape) - 1])
            return ap.rearrange(f"{lead} (g u s) -> {lead} g u s", g=STRIPS, u=TILES)[..., t, :]


        def ALL(ap):
            return ap

        HALF = [lambda ap, t=t: tile_cols(ap, t) for t in range(TILES)]

        jobs = []
        for n, q, k in TABLE_JOBS:
            src = tables[ONEHOT_TABLES[n]].rearrange("(p q) d -> p q d", q=CHUNKS[n])[:, q:q + k, :]
            at = slice((CHUNK0[n] + q) * D, (CHUNK0[n] + q + k) * D)
            jobs.append((src, VROWS, k * D, tab_hi[0:VROWS, at], tab_lo[0:VROWS, at]))
        jobs.append((w_pairs[:, 0:2, :], PCH, 2 * H1, wp_hi[0:PCH, 0:2 * H1], wp_lo[0:PCH, 0:2 * H1]))
        jobs.append((w_pairs[:, 2:NPCH, :], PCH, (NPCH - 2) * H1, wp_hi[0:PCH, 2 * H1:], wp_lo[0:PCH, 2 * H1:]))
        jobs.append((w2, P, M1 * H2, w2_hi[:, :], w2_lo[:, :]))
        jobs.append((w_dense, P, 2 * H1, wd_hi[:, :], wd_lo[:, :]))
        NJ = len(jobs)
        buf = [n % STAGES if n < NTJ else STAGES - 1 for n in range(NJ)]
        use = [buf[:n + 1].count(buf[n]) for n in range(NJ)]

        ident_zero, ident_made, row_ids_made = sem("ident_zero"), sem("ident_made"), sem("row_ids_made")
        idx_loaded = [sem(f"idx_loaded{t}") for t in range(TILES)]
        dense_loaded = [sem(f"dense_loaded{t}") for t in range(TILES)]
        gathered = [[sem(f"gathered{t}_{g}") for g in range(NTR)] for t in range(TILES)]
        tiles_begun = sem("tiles_begun")
        first_ids_loaded = sem("first_ids_loaded")
        ids_loaded = sem("ids_loaded")
        staged = [sem(f"staged{k}") for k in range(STAGES)]
        weights_loaded, wd_summed = sem("weights_loaded"), sem("wd_summed")
        hi_made, lo_made = sem("hi_made"), sem("lo_made")
        gram_cleared = sem("gram_cleared")
        onehot_made = sem("onehot_made")
        looked_up = sem("looked_up")
        lookup_copied = sem("lookup_copied")
        transposed = sem("transposed")
        tr_copied_act, tr_copied_dve = sem("tr_copied_act"), sem("tr_copied_dve")
        gram_done, gram_copied = sem("gram_done"), sem("gram_copied")
        scratch_written = sem("scratch_written")
        pairs_loaded = sem("pairs_loaded")
        tile_written = [sem(f"tile_written{t}") for t in range(TILES)]
        tile_loaded = [sem(f"tile_loaded{t}") for t in range(TILES)]
        pairs_hi_made, pairs_lo_made = sem("pairs_hi_made"), sem("pairs_lo_made")
        denseT_hi_made, denseT_lo_made = sem("denseT_hi_made"), sem("denseT_lo_made")
        l1_done, h1_hi_made, h1_lo_made = sem("l1_done"), sem("h1_hi_made"), sem("h1_lo_made")
        l2_done, h2_made = sem("l2_done"), sem("h2_made")
        y_done, y_copied = sem("y_done"), sem("y_copied")
        y_stored = sem("y_stored")

        block = ctx.enter_context(nc.Block())

        @block.sync
        def _(sp):
            def load_indices(tile, t):
                sp.dma_start(idx[t][:, :], ids_gather[tile, :, :]).then_inc(idx_loaded[t], 16)

            def load_dense(tile, t):
                sp.dma_start(rows[t][:, 0, :], dense[tile, :, :]).then_inc(dense_loaded[t], 16)

            def next_indices(m, t):
                for g in range(NTR):
                    sp.wait_ge(gathered[t][g], 16 * GATHERS[g] * m + 16 * GATHERS[g])
                load_indices((m + 1) * TILES + t, t)

            def next_dense(m, t):
                sp.wait_ge(transposed, 2 * NTR * m + NTR * (t + 1))
                load_dense((m + 1) * TILES + t, t)

            def load_ids(m):
                sp.dma_start(ids_b[:, :, :], ids_onehot[m, :, :].partition_broadcast(P)).then_inc(ids_loaded, 16)

            def gram_through_scratch(m):
                sp.wait_ge(gram_copied, 4 * m + 4)
                for g in range(STRIPS):
                    cols = slice(g * TILES * SS, (g + 1) * TILES * SS)
                    sp.dma_start(scratch_main(scratch, cols), gram[32 * g:32 * g + 32, :, :]) \
                      .then_inc(scratch_written, 16)
                    sp.dma_start(scratch_wrap(scratch, cols), gram[32 * g + N - NK:32 * g + N, 0:NK, :]) \
                      .then_inc(scratch_written, 16)
                sp.wait_ge(scratch_written, 32 * STRIPS * (m + 1))
                for k in range(NPCH):
                    sp.dma_start(pairs[0:PCH, k, :], scratch_pairs(scratch, k)).then_inc(pairs_loaded, 16)

            def tile_through_scratch(m, t):
                sp.wait_ge(gram_copied, 4 * m + 2 * t + 2)
                for g in range(STRIPS):
                    cols = slice(g * SS, (g + 1) * SS)
                    src = gram[:, :, t * SS:(t + 1) * SS]
                    sp.dma_start(scratch_main(scratch_of_tile[t], cols), src[32 * g:32 * g + 32]) \
                      .then_inc(tile_written[t], 16)
                    sp.dma_start(scratch_wrap(scratch_of_tile[t], cols), src[32 * g + N - NK:32 * g + N, 0:NK, :]) \
                      .then_inc(tile_written[t], 16)
                sp.wait_ge(tile_written[t], 32 * STRIPS)
                for k in range(NPCH):
                    sp.dma_start(pairs_of_tile[t][0:PCH, k, :], scratch_pairs(scratch_of_tile[t], k)) \
                      .then_inc(tile_loaded[t], 16)

            def store_y(m):
                sp.wait_ge(y_copied, m + 1)
                sp.dma_start(out[m, :, :], y[:, :]).then_inc(y_stored, 16)

            def stage_job(n):
                src, np_, width, _, _ = jobs[n]
                earlier = [k for k in range(n) if buf[k] == buf[n]]
                if earlier:
                    sp.wait_ge(hi_made, earlier[-1] + 1)
                    sp.wait_ge(lo_made, earlier[-1] + 1)
                dst = stage[buf[n]][0:np_, 0:width].rearrange("p (a b) -> p a b", a=src.shape[1])
                sp.dma_start(dst, src).then_inc(staged[buf[n]], 16)

            def macro(m, first):
                if not first:
                    sp.wait_ge(onehot_made, NO * m + NO)
                    load_ids(m + 1)
                    next_indices(m, 0)
                next_dense(m, 0)
                next_indices(m, 1)
                next_dense(m, 1)
                gram_through_scratch(m)
                if not first:
                    store_y(m - 1)

            for t in range(TILES):
                load_indices(t, t)
            sp.dma_start(ids_b[:, 0:2, :], ids_onehot[0, 0:2, :].partition_broadcast(P)).then_inc(first_ids_loaded, 16)
            for n in range(2):
                stage_job(n)
            sp.dma_start(ids_b[:, 2:NO, :], ids_onehot[0, 2:NO, :].partition_broadcast(P)).then_inc(ids_loaded, 16)
            for n in range(2, NTJ):
                stage_job(n)
                if n == STAGES:
                    for t in range(TILES):
                        load_dense(t, t)
            for dst, wsrc in ((w3s, w3), (b1s, b1), (b2s, b2)):
                sp.dma_start(dst[:, :], wsrc).then_inc(weights_loaded, 16)
            next_indices(0, 0)
            sp.wait_ge(onehot_made, NO)
            load_ids(1)
            for n in range(NTJ, NJ):
                stage_job(n)
            sp.wait_ge(lo_made, NJ)
            macro(0, True)
            with sp.Fori(1, MACROS - 1) as m:
                macro(m, False)
            store_y(MACROS - 2)
            for t in range(TILES):
                tile_through_scratch(MACROS - 1, t)
            sp.wait_ge(y_copied, MACROS + 1)
            sp.dma_start(out[MACROS - 1, :, :], y[:, :]).then_inc(y_stored, 16)
            sp.wait_ge(y_stored, 16 * MACROS)

        @block.gpsimd
        def _(pool):
            pool.memset(ident[:, :], 0.0).then_inc(ident_zero, 1)
            for ch, ids in row_id.items():
                pool.iota(ids[:, :], [[1, ch]], 0, ch).then_inc(row_ids_made, 1)
            pool.wait_ge(ident_zero, 1)
            pool.affine_select(out=ident[:, :], in_=ident[:, :], compare_op=ALU.not_equal, fill=1.0,
                               base=0, pattern=[[-1, P]], channel_multiplier=1).then_inc(ident_made, 1)

            def gather_tile(m, t, first):
                pool.wait_ge(idx_loaded[t], 16 * m + 16)
                if not first:
                    pool.wait_ge(transposed, 2 * NTR * (m - 1) + NTR * (t + 1))
                pool.sem_inc(tiles_begun, 1)
                for n, f in enumerate(GATHER_TABLES):
                    group = (1 + n) // 4
                    pool.indirect_dma_start(
                        out=rows[t][:, 1 + n, :], out_offset=None, in_=tables[f],
                        in_offset=bass.IndirectOffsetOnAxis(ap=idx[t][:, n:n + 1], axis=0),
                    ).then_inc(gathered[t][group], 16)

            for t in range(TILES):
                gather_tile(0, t, True)
            with pool.Fori(1, MACROS) as m:
                for t in range(TILES):
                    gather_tile(m, t, False)

        @block.tensor
        def _(pe):
            def transpose_group(m, t, g, first):
                f0, nf = TR_GROUPS[g]
                if g == 0:
                    pe.wait_ge(dense_loaded[t], 16 * m + 16)
                pe.wait_ge(gathered[t][g], 16 * GATHERS[g] * m + 16 * GATHERS[g])
                if g % 2 == 0:
                    n = TR_ACT * t + g // 2
                    if not (first and n == 0):
                        pe.wait_ge(tr_copied_act, 2 * TR_ACT * m + n)
                else:
                    n = TR_DVE * t + g // 2
                    if not (first and n == 0):
                        pe.wait_ge(tr_copied_dve, 2 * TR_DVE * m + n)
                for k in range(nf):
                    last = pe.transpose(TR[g % 2][:, k * P:(k + 1) * P], rows[t][:, f0 + k, :], ident[:, :])
                last.then_inc(transposed, 1)

            def lookup(m, n, first):
                b = n % 2
                pe.wait_ge(onehot_made, NO * m + n + 1)
                if not (first and n < 2):
                    pe.wait_ge(lookup_copied, NO * m + n - 1)
                if first:
                    pe.wait_ge(hi_made, JOBS_AFTER[n])
                    pe.wait_ge(lo_made, JOBS_AFTER[n])
                for q in range(CHUNKS[n]):
                    at = slice((CHUNK0[n] + q) * D, (CHUNK0[n] + q + 1) * D)
                    pe.matmul(OH[b][:, 0:MC], tab_hi[0:VROWS, at], onehot[n % ONEHOTS][0:VROWS, q, :],
                              start=(q == 0), stop=False)
                    last = pe.matmul(OH[b][:, 0:MC], tab_lo[0:VROWS, at], onehot[n % ONEHOTS][0:VROWS, q, :],
                                     start=False, stop=(q == CHUNKS[n] - 1))
                last.then_inc(looked_up, 1)

            def gram_half(m, t, b, half, first):
                if half == 0:
                    if not (first and t == 0):
                        pe.wait_ge(gram_copied, 4 * m + 2 * t + b - 1)
                    if t == 0 and b == 0:
                        pe.wait_ge(lookup_copied, NO * m + NO)
                    if b == 0:
                        pe.wait_ge(tr_copied_act, 2 * TR_ACT * m + TR_ACT * (t + 1))
                        pe.wait_ge(tr_copied_dve, 2 * TR_DVE * m + TR_DVE * (t + 1))
                    if first and t == 0 and b == 0:
                        pe.wait_ge(gram_cleared, 2)
                hs = BANK_SAMPLES // 2
                for s in range(half * hs, (half + 1) * hs):
                    for g in range(STRIPS):
                        c = (g * TILES + t) * SS + b * BANK_SAMPLES + s
                        last = pe.matmul(GR[b][32 * g:32 * g + N, s * N:(s + 1) * N], ET[:, c, :], ET[:, c, :],
                                         start=True, stop=True)
                if half == 1:
                    last.then_inc(gram_done, 1)

            def split_products(out, terms):
                n = 0
                for w_hi, w_lo, x_hi, x_lo in terms:
                    for w, x in ((w_hi, x_hi), (w_hi, x_lo), (w_lo, x_hi)):
                        last = pe.matmul(out, w, x, start=(n == 0), stop=(n == 3 * len(terms) - 1))
                        n += 1
                return last

            def layer1(u, c, cols, first):
                if c == 0:
                    pe.wait_ge(pairs_lo_made, u + 1)
                    pe.wait_ge(denseT_lo_made, u + 1)
                    if first:
                        pe.wait_ge(hi_made, NJ)
                        pe.wait_ge(lo_made, NJ)
                    else:
                        pe.wait_ge(y_copied, u)
                elif c == 1:
                    if not first:
                        pe.wait_ge(h2_made, M2 * u)
                else:
                    pe.wait_ge(h1_hi_made, M1 * u + c - 1)
                terms = [(wd_hi[:, c * P:(c + 1) * P], wd_lo[:, c * P:(c + 1) * P],
                          cols(denseT_hi[:, :]), cols(denseT_lo[:, :]))]
                for k in range(NPCH):
                    at = slice(k * H1 + c * P, k * H1 + (c + 1) * P)
                    terms.append((wp_hi[0:PCH, at], wp_lo[0:PCH, at], cols(pairs_hi[0:PCH, k, :]), cols(pairs_lo[0:PCH, k, :])))
                split_products(cols(ML[c % 2][:, 0:MC]), terms).then_inc(l1_done, 1)

            def layer2(u, c, cols):
                pe.wait_ge(h1_lo_made, M1 * u + M1)
                terms = []
                for k in range(M1):
                    at = slice(k * H2 + c * P, k * H2 + (c + 1) * P)
                    terms.append((w2_hi[:, at], w2_lo[:, at], cols(h1_hi[:, k, :]), cols(h1_lo[:, k, :])))
                split_products(cols(ML[c % 2][:, 0:MC]), terms).then_inc(l2_done, 1)

            def layer3(u, tiles, first):
                if first:
                    pe.wait_ge(weights_loaded, 16 * 3)
                pe.wait_ge(h2_made, M2 * u + M2)
                for a in tiles:
                    for k in range(M2):
                        last = pe.matmul(ML[0][:, a:a + 1], h2[:, k, a, :], w3s[:, k:k + 1],
                                         start=(k == 0), stop=(k == M2 - 1))
                last.then_inc(y_done, 1)

            def gram_bank(m, t, b, first):
                for half in range(2):
                    gram_half(m, t, b, half, first)

            def lookups_and_tile0(m, first, mlp):
                for n in range(NO - 2):
                    lookup(m, n, first)
                if first:
                    pe.wait_ge(ident_made, 1)
                transpose_group(m, 0, 0, first)
                transpose_group(m, 0, 1, first)
                lookup(m, NO - 2, first)
                transpose_group(m, 0, 2, first)
                transpose_group(m, 0, 3, first)
                lookup(m, NO - 1, first)
                for g in range(4, NTR):
                    transpose_group(m, 0, g, first)
                if mlp:
                    layer1(m - 1, 0, ALL, mlp == "first")
                    layer1(m - 1, 1, ALL, mlp == "first")
                gram_bank(m, 0, 0, first)
                if mlp:
                    layer1(m - 1, 2, ALL, mlp == "first")
                    layer1(m - 1, 3, ALL, mlp == "first")

            def tile1(m, first, mlp):
                gram_half(m, 0, 1, 0, first)
                transpose_group(m, 1, 0, first)
                transpose_group(m, 1, 1, first)
                gram_half(m, 0, 1, 1, first)
                transpose_group(m, 1, 2, first)
                transpose_group(m, 1, 3, first)
                if mlp:
                    layer2(m - 1, 0, ALL)
                for g in range(4, NTR):
                    transpose_group(m, 1, g, first)
                if mlp:
                    layer2(m - 1, 1, ALL)
                gram_bank(m, 1, 0, first)
                gram_bank(m, 1, 1, first)
                if mlp:
                    layer3(m - 1, range(MC // P), mlp == "first")

            lookups_and_tile0(0, True, None)
            tile1(0, True, None)
            lookups_and_tile0(1, False, "first")
            tile1(1, False, "first")
            with pe.Fori(2, MACROS - 1) as m:
                lookups_and_tile0(m, False, "later")
                tile1(m, False, "later")

            lookups_and_tile0(LAST, False, "later")
            gram_bank(LAST, 0, 1, False)
            for c in range(M2):
                layer2(LAST - 1, c, ALL)
            layer3(LAST - 1, range(MC // P), False)
            for t in range(TILES):
                if t == 1:
                    for g in range(NTR):
                        transpose_group(LAST, 1, g, False)
                    for b in range(2):
                        gram_bank(LAST, 1, b, False)
                    for n in range(WARM):
                        pe.matmul(OH[0][:, 0:MC], tab_hi[0:VROWS, 0:P], onehot[0][0:VROWS, 0, :], start=True, stop=True)
                for c in range(M1):
                    layer1(LAST + t, c, HALF[t], False)
                for c in range(M2):
                    layer2(LAST + t, c, HALF[t])
                layer3(LAST + t, [t], False)

        def et_tile(t, f0, nf):
            return ET[:, :, f0:f0 + nf].rearrange("p (g u s) f -> p u f g s", g=STRIPS, u=TILES)[:, t]

        def copy_group(copy, t, g):
            f0, nf = TR_GROUPS[g]
            return copy(et_tile(t, DENSE_SLOT + f0, nf),
                        TR[g % 2][:, 0:nf * P].rearrange("p (f g s) -> p f g s", g=STRIPS, s=SS))

        @block.scalar
        def _(act):
            def copy_lookup(m, n):
                act.wait_ge(looked_up, NO * m + n + 1)
                act.copy(ET[:, :, n], OH[n % 2][:, 0:MC]).then_inc(lookup_copied, 1)

            def copy_transposed(m, t, g, first=False):
                if t == 0 and g == 0 and not first:
                    act.wait_ge(denseT_lo_made, m)
                act.wait_ge(transposed, 2 * NTR * m + NTR * t + g + 1)
                copy_group(act.copy, t, g).then_inc(tr_copied_act, 1)

            def make_pairs_hi(m):
                act.wait_ge(pairs_loaded, 16 * NPCH * m + 16 * NPCH)
                act.copy(pairs_hi[0:PCH, :, :], pairs[0:PCH, :, :]).then_inc(pairs_hi_made, 1)

            def make_pairs_hi_of_tile(t):
                act.wait_ge(tile_loaded[t], 16 * NPCH)
                act.copy(HALF[t](pairs_hi[0:PCH, :, :]),
                         pairs_of_tile[t][0:PCH].rearrange("p k (g s) -> p k g s", g=STRIPS)).then_inc(pairs_hi_made, 1)

            def make_h1(u, c, cols, first):
                act.wait_ge(l1_done, M1 * u + c + 1)
                if not (first and c < 2):
                    act.wait_ge(h1_lo_made, M1 * u + c - 1)
                if first and c == 0:
                    act.wait_ge(weights_loaded, 16 * 3)
                act.activation(cols(h1f[c % 2]), cols(ML[c % 2][:, 0:MC]), ACT.Relu, bias=b1s[:, c:c + 1])
                act.activation(cols(h1_hi[:, c, :]), cols(ML[c % 2][:, 0:MC]), ACT.Relu, bias=b1s[:, c:c + 1]) \
                   .then_inc(h1_hi_made, 1)

            def copy_gram(m, t, b, first):
                act.wait_ge(gram_done, 4 * m + 2 * t + b + 1)
                if t == 0 and b == 0:
                    if first:
                        act.wait_ge(hi_made, NTJ)
                        act.wait_ge(lo_made, NTJ)
                    else:
                        act.wait_ge(scratch_written, 32 * STRIPS * m)
                s0 = t * SS + b * BANK_SAMPLES
                act.copy(gram[:, :, s0:s0 + BANK_SAMPLES],
                         GR[b][:, 0:BANK_SAMPLES * N].rearrange("p (s j) -> p j s", j=N)).then_inc(gram_copied, 1)

            def make_h2(u, c, tiles):
                act.wait_ge(l2_done, M2 * u + c + 1)
                for t in tiles:
                    last = act.activation(h2[:, c, t, :].rearrange("p (g s) -> p g s", g=STRIPS), HALF[t](ML[c % 2][:, 0:MC]),
                                          ACT.Relu, bias=b2s[:, c:c + 1])
                last.then_inc(h2_made, 1)

            def copy_y(u, tiles, first):
                act.wait_ge(y_done, u + 1)
                if not first and tiles[0] == 0:
                    act.wait_ge(y_stored, 16 * u)
                act.copy(y[:, tiles[0]:tiles[-1] + 1], ML[0][:, tiles[0]:tiles[-1] + 1]).then_inc(y_copied, 1)

            def make_denseT_hi(m, u, cols, t):
                act.wait_ge(tr_copied_act, 2 * TR_ACT * m + TR_ACT * t + 1)
                act.copy(cols(denseT_hi[:, :]), cols(ET[:, :, DENSE_SLOT])).then_inc(denseT_hi_made, 1)

            def split_hi(n):
                _, np_, width, hi, _ = jobs[n]
                if n == NJ - 1:
                    act.wait_ge(wd_summed, 1)
                    width = H1
                else:
                    act.wait_ge(staged[buf[n]], 16 * use[n])
                act.copy(hi, stage[buf[n]][0:np_, 0:width]).then_inc(hi_made, 1)

            def lookups_and_tile0(m, first, mlp):
                for n in range(NO - 2):
                    if first and n + 2 < NTJ:
                        split_hi(n + 2)
                    copy_lookup(m, n)
                copy_transposed(m, 0, 0, first)
                if mlp:
                    make_pairs_hi(m - 1)
                copy_lookup(m, NO - 2)
                copy_transposed(m, 0, 2)
                copy_lookup(m, NO - 1)
                for g in range(4, NTR, 2):
                    copy_transposed(m, 0, g)
                if mlp:
                    make_h1(m - 1, 0, ALL, mlp == "first")
                    make_h1(m - 1, 1, ALL, mlp == "first")
                copy_gram(m, 0, 0, first)
                if mlp:
                    make_h1(m - 1, 2, ALL, mlp == "first")
                    make_h1(m - 1, 3, ALL, mlp == "first")

            def tile1(m, first, mlp):
                if first:
                    split_hi(NTJ)
                copy_transposed(m, 1, 0)
                copy_gram(m, 0, 1, first)
                copy_transposed(m, 1, 2)
                if first:
                    split_hi(NTJ + 1)
                if mlp:
                    make_h2(m - 1, 0, range(TILES))
                for g in range(4, NTR, 2):
                    copy_transposed(m, 1, g)
                if mlp:
                    make_h2(m - 1, 1, range(TILES))
                make_denseT_hi(m, m, ALL, 1)
                copy_gram(m, 1, 0, first)
                if first:
                    split_hi(NTJ + 2)
                copy_gram(m, 1, 1, first)
                if first:
                    split_hi(NTJ + 3)
                if mlp:
                    copy_y(m - 1, range(MC // P), mlp == "first")

            def mlp_of_tile(u, t):
                make_pairs_hi_of_tile(t)
                for c in range(M1):
                    make_h1(u, c, HALF[t], False)
                for c in range(M2):
                    make_h2(u, c, [t])
                copy_y(u, [t], False)

            split_hi(0)
            split_hi(1)
            lookups_and_tile0(0, True, None)
            tile1(0, True, None)
            lookups_and_tile0(1, False, "first")
            tile1(1, False, "first")
            with act.Fori(2, MACROS - 1) as m:
                lookups_and_tile0(m, False, "later")
                tile1(m, False, "later")

            lookups_and_tile0(LAST, False, "later")
            copy_gram(LAST, 0, 1, False)
            make_denseT_hi(LAST, LAST, HALF[0], 0)
            for c in range(M2):
                make_h2(LAST - 1, c, range(TILES))
            copy_y(LAST - 1, range(MC // P), False)
            mlp_of_tile(LAST, 0)
            for g in range(0, NTR, 2):
                copy_transposed(LAST, 1, g)
            make_denseT_hi(LAST, LAST + 1, HALF[1], 1)
            for b in range(2):
                copy_gram(LAST, 1, b, False)
            mlp_of_tile(LAST + 1, 1)

        @block.vector
        def _(dve):
            def make_onehot(m, n, first):
                if first and n == 0:
                    dve.wait_ge(first_ids_loaded, 16)
                if n == (2 if first else 0):
                    dve.wait_ge(ids_loaded, 16 * m + 16)
                if not (first and n < ONEHOTS):
                    dve.wait_ge(looked_up, NO * m + n - ONEHOTS + 1)
                ch = CHUNKS[n]
                dve.tensor_tensor(
                    onehot[n % ONEHOTS][0:VROWS, 0:ch, :],
                    ids_b[0:VROWS, n, :].unsqueeze(1).to_broadcast([VROWS, ch, MC]),
                    row_id[ch][0:VROWS, :].unsqueeze(2).to_broadcast([VROWS, ch, MC]),
                    ALU.is_equal).then_inc(onehot_made, 1)

            def copy_transposed(m, t, g):
                dve.wait_ge(transposed, 2 * NTR * m + NTR * t + g + 1)
                copy_group(dve.tensor_copy, t, g).then_inc(tr_copied_dve, 1)

            def make_pairs_lo(m):
                dve.wait_ge(pairs_hi_made, m + 1)
                dve.tensor_tensor(pairs_lo[0:PCH, :, :], pairs[0:PCH, :, :], pairs_hi[0:PCH, :, :].bitcast(F32),
                                  ALU.subtract).then_inc(pairs_lo_made, 1)

            def make_pairs_lo_of_tile(u, t):
                dve.wait_ge(pairs_hi_made, u + 1)
                dve.tensor_tensor(HALF[t](pairs_lo[0:PCH, :, :]),
                                  pairs_of_tile[t][0:PCH].rearrange("p k (g s) -> p k g s", g=STRIPS),
                                  HALF[t](pairs_hi[0:PCH, :, :].bitcast(F32)), ALU.subtract).then_inc(pairs_lo_made, 1)

            def make_denseT_lo(u, cols):
                dve.wait_ge(denseT_hi_made, u + 1)
                dve.tensor_tensor(cols(denseT_lo[:, :]), cols(ET[:, :, DENSE_SLOT]), cols(denseT_hi[:, :].bitcast(F32)),
                                  ALU.subtract).then_inc(denseT_lo_made, 1)

            def make_h1_lo(u, c, cols):
                dve.wait_ge(h1_hi_made, M1 * u + c + 1)
                dve.tensor_tensor(cols(h1_lo[:, c, :]), cols(h1f[c % 2]), cols(h1_hi[:, c, :].bitcast(F32)),
                                  ALU.subtract).then_inc(h1_lo_made, 1)

            def split_lo(n):
                _, np_, width, hi, lo = jobs[n]
                if n == NJ - 1:
                    dve.wait_ge(staged[buf[n]], 16 * use[n])
                    width = H1
                    st = stage[buf[n]]
                    dve.tensor_tensor(st[:, 0:H1], st[:, 0:H1], st[:, H1:2 * H1], ALU.add).then_inc(wd_summed, 1)
                dve.wait_ge(hi_made, n + 1)
                dve.tensor_tensor(lo, stage[buf[n]][0:np_, 0:width], hi.bitcast(F32),
                                  ALU.subtract).then_inc(lo_made, 1)

            for b in range(2):
                dve.memset(GR[b][:, :], 0.0).then_inc(gram_cleared, 1)
            dve.wait_ge(row_ids_made, len(row_id))
            make_onehot(0, 0, True)
            make_onehot(0, 1, True)
            for n in range(NO):
                for k in range(JOBS_AFTER[n - 1] if n else 0, JOBS_AFTER[n]):
                    split_lo(k)
                if n >= 2:
                    make_onehot(0, n, True)
                if n == NO - 2:
                    copy_transposed(0, 0, 1)
            copy_transposed(0, 0, 3)
            split_lo(NTJ)
            copy_transposed(0, 1, 1)
            split_lo(NTJ + 1)
            copy_transposed(0, 1, 3)
            make_denseT_lo(0, ALL)
            make_onehot(1, 0, False)
            split_lo(NTJ + 2)
            make_onehot(1, 1, False)
            split_lo(NTJ + 3)
            make_onehot(1, 2, False)
            make_onehot(1, 3, False)

            def macro(m, last):
                for n in range(ONEHOTS, NO):
                    make_onehot(m, n, False)
                copy_transposed(m, 0, 1)
                make_pairs_lo(m - 1)
                copy_transposed(m, 0, 3)
                make_h1_lo(m - 1, 0, ALL)
                make_h1_lo(m - 1, 1, ALL)
                if not last:
                    make_onehot(m + 1, 0, False)
                make_h1_lo(m - 1, 2, ALL)
                make_h1_lo(m - 1, 3, ALL)
                if not last:
                    copy_transposed(m, 1, 1)
                    make_onehot(m + 1, 1, False)
                    copy_transposed(m, 1, 3)
                    make_denseT_lo(m, ALL)
                    for n in range(2, ONEHOTS):
                        make_onehot(m + 1, n, False)

            def mlp_of_tile(u, t):
                make_pairs_lo_of_tile(u, t)
                for c in range(M1):
                    make_h1_lo(u, c, HALF[t])

            with dve.Fori(1, LAST) as m:
                macro(m, False)

            macro(LAST, True)
            make_denseT_lo(LAST, HALF[0])
            mlp_of_tile(LAST, 0)
            copy_transposed(LAST, 1, 1)
            copy_transposed(LAST, 1, 3)
            make_denseT_lo(LAST + 1, HALF[1])
            mlp_of_tile(LAST + 1, 1)


def _pair_rows():
    found = []
    for i in range(N):
        for k in range(1, NK + 1):
            a, b = sorted((SLOT_FEATURE[i], SLOT_FEATURE[(i + k) % N]))
            found.append(D + a * N - a * (a + 1) // 2 + b - a - 1)
    return np.array(found)


def kernel(**inputs):
    import concourse.bacc as bacc
    from concourse.bass_utils import run_bass_kernel_spmd

    def tiled(a):
        a = a.reshape(MACROS, STRIPS, TILES, SS, a.shape[1]).transpose(0, 2, 1, 3, 4)
        return a.reshape(MACROS * TILES, P, a.shape[-1])

    ids = np.asarray(inputs["ids"])
    w_top1 = np.asarray(inputs["W_top1"])
    ends = w_top1.shape[0] - D
    arrays = {
        "dense": tiled(np.asarray(inputs["r_dense_features"])),
        "ids_gather": tiled(ids[:, GATHER_TABLES]),
        "ids_onehot": ids[:, ONEHOT_TABLES].reshape(MACROS, MC, NO).transpose(0, 2, 1),
        "w_dense": np.stack([w_top1[0:D], w_top1[ends:ends + D]], axis=1),
        "w_pairs": w_top1[_pair_rows()].reshape(NPCH, PCH, H1).transpose(1, 0, 2),
        "b1": np.asarray(inputs["b_top1"]).reshape(M1, P).T,
        "w2": np.asarray(inputs["W_top2"]).reshape(M1, P, H2).transpose(1, 0, 2),
        "b2": np.asarray(inputs["b_top2"]).reshape(M2, P).T,
        "w3": np.asarray(inputs["W_top3"]).reshape(M2, P).T,
    }
    for f in range(FIELDS):
        arrays[f"tbl_{f}"] = np.asarray(inputs[f"tbl_{f}"])
    arrays = {name: np.ascontiguousarray(a) for name, a in arrays.items()}

    nc = bacc.Bacc("TRN2", target_bir_lowering=False, num_devices=1)
    aps = {name: nc.dram_tensor(name, a.shape, mybir.dt.from_np(a.dtype), kind="ExternalInput").ap()
           for name, a in arrays.items()}
    out = nc.dram_tensor("out", (MACROS, P, MC // P), mybir.dt.float32, kind="ExternalOutput").ap()
    build(nc, aps["dense"], aps["ids_gather"], aps["ids_onehot"], [aps[f"tbl_{f}"] for f in range(FIELDS)],
          aps["w_dense"], aps["w_pairs"], aps["b1"], aps["w2"], aps["b2"], aps["w3"], out)
    r = run_bass_kernel_spmd(nc, [arrays], core_ids=[0])
    y = r.results[0]["out"].reshape(MACROS, STRIPS, SS, TILES)
    return y.transpose(0, 1, 3, 2).reshape(BATCH, 1)
```

```python
from contextlib import ExitStack

import concourse.bass as bass
import numpy as np
from concourse import mybir

BATCH, FIELDS, D = 2048, 26, 128
VOCABS = [12500, 12500, 1250, 1000, 125000, 1000, 1000, 1000, 1250, 1250, 12500, 12500, 12500,
          1250, 12500, 1250, 1250, 1000, 1000, 1250, 1250, 1000, 12500, 1000, 12500, 1250]
H1, H2 = 512, 256
P = 128

WARM = 48
ONEHOTS = 4
ONEHOT_TABLES = [f for f, v in enumerate(VOCABS) if v == min(VOCABS)]
GATHER_TABLES = [f for f in range(FIELDS) if f not in ONEHOT_TABLES]
NO, NG = len(ONEHOT_TABLES), len(GATHER_TABLES)
CHUNKS = -(-min(VOCABS) // P)
VROWS = min(VOCABS) // CHUNKS
TABLE = CHUNKS * D
assert VROWS * CHUNKS == min(VOCABS)

N = FIELDS + 1
NK = N // 2
NCOL = N - 1
SLOT_FEATURE = [1 + f for f in ONEHOT_TABLES] + [0] + [1 + f for f in GATHER_TABLES]
DENSE_SLOT = NO
ROWS_IN = 1 + NG

MC = 256
MACROS = BATCH // MC
TILES = 2
STRIPS = 4
SS = P // STRIPS
BANK_SAMPLES = 16
TR_GROUPS = [(g, min(4, ROWS_IN - g)) for g in range(0, ROWS_IN, 4)]
NTR = len(TR_GROUPS)
TR_ACT = len(TR_GROUPS[0::2])
TR_DVE = len(TR_GROUPS[1::2])
GATHERS = [nf - (f0 == 0) for f0, nf in TR_GROUPS]
ICH = 9
PCH = ICH * NK
NPCH = N // ICH
M1, M2 = H1 // P, H2 // P
LOADS = NPCH + 1
LAST = MACROS - 1
STAGES = 3
STAGE = 1024


def build(nc, dense, ids_gather, ids_onehot, tables, w_dense, w_pairs, b1, w2, b2, w3, out):
    F32, F32R, I32 = mybir.dt.float32, mybir.dt.float32r, mybir.dt.int32
    ALU = mybir.AluOpType
    ACT = mybir.ActivationFunctionType

    ctx = ExitStack()
    with ctx:
        def sb(name, shape, dt=F32):
            return ctx.enter_context(nc.sbuf_tensor(name, shape, dt))

        def bank(name):
            return ctx.enter_context(nc.psum_tensor(name, [P, 512], F32))

        def sem(name):
            return ctx.enter_context(nc.semaphore(name))

        rows = [sb(f"rows{t}", [P, ROWS_IN, D]) for t in range(TILES)]
        idx = [sb(f"idx{t}", [P, NG], I32) for t in range(TILES)]
        ET = sb("ET", [P, MC, N])
        tab_hi = sb("tab_hi", [P, NO * TABLE], F32R)
        tab_lo = sb("tab_lo", [P, NO * TABLE], F32R)
        onehot = [sb(f"onehot{k}", [P, CHUNKS, MC], F32R) for k in range(ONEHOTS)]
        ids_b = sb("ids_b", [P, NO, MC], I32)
        row_id = sb("row_id", [P, CHUNKS], I32)
        early = sb("early", [P, STAGES * STAGE])
        stage = [early[:, k * STAGE:(k + 1) * STAGE] for k in range(STAGES)]
        GRAM, PAIRS = NCOL * TILES * SS, NPCH * MC
        gram = early[:, 0:GRAM].rearrange("p (j c) -> p j c", j=NCOL)
        pairs = early[:, GRAM:GRAM + PAIRS].rearrange("p (k c) -> p k c", k=NPCH)
        h1f = [early[:, GRAM + PAIRS + k * MC:GRAM + PAIRS + (k + 1) * MC] for k in range(2)]
        pairs_hi = sb("pairs_hi", [P, NPCH, MC], F32R)
        pairs_lo = sb("pairs_lo", [P, NPCH, MC], F32R)
        denseT_hi = sb("denseT_hi", [P, MC], F32R)
        denseT_lo = sb("denseT_lo", [P, MC], F32R)
        wd_hi, wd_lo = sb("wd_hi", [P, H1], F32R), sb("wd_lo", [P, H1], F32R)
        wp_hi, wp_lo = sb("wp_hi", [P, NPCH * H1], F32R), sb("wp_lo", [P, NPCH * H1], F32R)
        w2_hi, w2_lo = sb("w2_hi", [P, M1 * H2], F32R), sb("w2_lo", [P, M1 * H2], F32R)
        w3s = sb("w3s", [P, M2])
        b1s = sb("b1s", [P, M1])
        b2s = sb("b2s", [P, M2])
        h1_hi = sb("h1_hi", [P, M1, MC], F32R)
        h1_lo = sb("h1_lo", [P, M1, MC], F32R)
        h2 = sb("h2", [P, M2, MC])
        y = sb("y", [P, MC // P])
        ident = sb("ident", [P, P])

        TR = [bank("tr_even"), bank("tr_odd")]
        OH = [bank("oh_a"), bank("oh_b")]
        GR = [bank("gr_a"), bank("gr_b")]
        ML = [bank("mlp_a"), bank("mlp_b")]
        LAST_L1, LAST_L2 = ML + GR, TR

        scratch = nc.dram_tensor("scratch", [32 * NCOL, MC], F32, kind="Internal").ap()

        entries = scratch[0:(N - 1) * N, :].rearrange("(i k) c -> i k c", k=N)[:, 1:1 + NK, :]
        pair_loads = []
        for k in range(NPCH):
            i0, i1 = k * ICH, min((k + 1) * ICH, N - 1)
            pair_loads.append((k, slice(0, (i1 - i0) * NK), entries[i0:i1, :, :]))
        pair_loads.append((NPCH - 1, slice(PCH - NK, PCH), scratch[(N - 1) * NCOL + NK:N * NCOL, :]))

        jobs = []
        for n, f in enumerate(ONEHOT_TABLES):
            at = slice(n * TABLE, (n + 1) * TABLE)
            jobs.append((tables[f].rearrange("(p q) d -> p q d", q=CHUNKS), VROWS, TABLE,
                         tab_hi[0:VROWS, at], tab_lo[0:VROWS, at]))
        jobs.append((w_pairs[:, 0:2, :], PCH, 2 * H1, wp_hi[0:PCH, 0:2 * H1], wp_lo[0:PCH, 0:2 * H1]))
        jobs.append((w_pairs[:, 2:NPCH, :], PCH, (NPCH - 2) * H1, wp_hi[0:PCH, 2 * H1:], wp_lo[0:PCH, 2 * H1:]))
        jobs.append((w2, P, M1 * H2, w2_hi[:, :], w2_lo[:, :]))
        jobs.append((w_dense, P, 2 * H1, wd_hi[:, :], wd_lo[:, :]))
        NJOBS = len(jobs)
        buf = [n % STAGES if n < NO else STAGES - 1 for n in range(NJOBS)]
        use = [buf[:n + 1].count(buf[n]) for n in range(NJOBS)]

        ident_zero, ident_made, row_ids_made = sem("ident_zero"), sem("ident_made"), sem("row_ids_made")
        idx_loaded = [sem(f"idx_loaded{t}") for t in range(TILES)]
        dense_loaded = [sem(f"dense_loaded{t}") for t in range(TILES)]
        gathered = [[sem(f"gathered{t}_{g}") for g in range(NTR)] for t in range(TILES)]
        tiles_begun = sem("tiles_begun")
        first_ids_loaded = sem("first_ids_loaded")
        ids_loaded = sem("ids_loaded")
        staged = [sem(f"staged{k}") for k in range(STAGES)]
        weights_loaded, wd_summed = sem("weights_loaded"), sem("wd_summed")
        hi_made, lo_made = sem("hi_made"), sem("lo_made")
        gram_cleared = sem("gram_cleared")
        onehot_made = sem("onehot_made")
        looked_up = sem("looked_up")
        lookup_copied = sem("lookup_copied")
        transposed = sem("transposed")
        tr_copied_act, tr_copied_dve = sem("tr_copied_act"), sem("tr_copied_dve")
        gram_done, gram_copied = sem("gram_done"), sem("gram_copied")
        scratch_written = sem("scratch_written")
        pairs_loaded = sem("pairs_loaded")
        last_pairs_loaded = [sem(f"last_pairs_loaded{k}") for k in range(NPCH)]
        pairs_hi_made, pairs_lo_made = sem("pairs_hi_made"), sem("pairs_lo_made")
        denseT_hi_made, denseT_lo_made = sem("denseT_hi_made"), sem("denseT_lo_made")
        l1_done, h1_hi_made, h1_lo_made = sem("l1_done"), sem("h1_hi_made"), sem("h1_lo_made")
        l2_done, h2_made = sem("l2_done"), sem("h2_made")
        y_done, y_copied = sem("y_done"), sem("y_copied")
        y_stored = sem("y_stored")

        block = ctx.enter_context(nc.Block())

        @block.sync
        def _(sp):
            def load_indices(tile, t):
                sp.dma_start(idx[t][:, :], ids_gather[tile, :, :]).then_inc(idx_loaded[t], 16)

            def load_dense(tile, t):
                sp.dma_start(rows[t][:, 0, :], dense[tile, :, :]).then_inc(dense_loaded[t], 16)

            def next_indices(m, t):
                for g in range(NTR):
                    sp.wait_ge(gathered[t][g], 16 * GATHERS[g] * m + 16 * GATHERS[g])
                load_indices((m + 1) * TILES + t, t)

            def next_dense(m, t):
                sp.wait_ge(transposed, 2 * NTR * m + NTR * (t + 1))
                load_dense((m + 1) * TILES + t, t)

            def load_ids(m):
                sp.dma_start(ids_b[:, :, :], ids_onehot[m, :, :].partition_broadcast(P)).then_inc(ids_loaded, 16)

            def write_gram(cols):
                for g in range(STRIPS):
                    strip = scratch[:, g * TILES * SS:(g + 1) * TILES * SS]
                    sp.dma_start(strip[:, cols].rearrange("(i j) c -> i j c", j=NCOL),
                                 gram[32 * g:32 * g + 32, :, cols]).then_inc(scratch_written, 16)

            def gram_through_scratch(m):
                sp.wait_ge(gram_copied, 4 * m + 4)
                write_gram(slice(0, TILES * SS))
                sp.wait_ge(scratch_written, 16 * STRIPS * m + 16 * STRIPS)
                for k, parts, src in pair_loads:
                    sp.dma_start(pairs[parts, k, :], src).then_inc(pairs_loaded, 16)

            def store_y(m):
                sp.wait_ge(y_copied, m + 1)
                sp.dma_start(out[m, :, :], y[:, :]).then_inc(y_stored, 16)

            def stage_job(n):
                src, parts, width, _, _ = jobs[n]
                earlier = [k for k in range(n) if buf[k] == buf[n]]
                if earlier:
                    sp.wait_ge(hi_made, earlier[-1] + 1)
                    sp.wait_ge(lo_made, earlier[-1] + 1)
                dst = stage[buf[n]][0:parts, 0:width].rearrange("p (a b) -> p a b", a=src.shape[1])
                sp.dma_start(dst, src).then_inc(staged[buf[n]], 16)

            def next_rows(m):
                next_dense(m, 0)
                next_indices(m, 1)

            def macro(m):
                sp.wait_ge(onehot_made, NO * m + NO)
                load_ids(m + 1)
                next_indices(m, 0)
                next_rows(m)
                next_dense(m, 1)
                gram_through_scratch(m)
                store_y(m - 1)

            for t in range(TILES):
                load_indices(t, t)
            sp.dma_start(ids_b[:, 0:2, :], ids_onehot[0, 0:2, :].partition_broadcast(P)).then_inc(first_ids_loaded, 16)
            for n in range(2):
                stage_job(n)
            sp.dma_start(ids_b[:, 2:NO, :], ids_onehot[0, 2:NO, :].partition_broadcast(P)).then_inc(ids_loaded, 16)
            for n in range(2, NO):
                stage_job(n)
                if n == STAGES:
                    for t in range(TILES):
                        load_dense(t, t)
            for dst, wsrc in ((w3s, w3), (b1s, b1), (b2s, b2)):
                sp.dma_start(dst[:, :], wsrc).then_inc(weights_loaded, 16)
            next_indices(0, 0)
            sp.wait_ge(onehot_made, NO)
            load_ids(1)
            stage_job(NO)
            next_rows(0)
            for n in range(NO + 1, NJOBS):
                stage_job(n)
            sp.wait_ge(lo_made, NJOBS)
            next_dense(0, 1)
            gram_through_scratch(0)
            with sp.Fori(1, LAST) as m:
                macro(m)
            sp.wait_ge(pairs_loaded, 16 * LOADS * LAST)
            for t in range(TILES):
                sp.wait_ge(gram_copied, 4 * LAST + 2 * t + 2)
                write_gram(slice(t * SS, (t + 1) * SS))
            sp.wait_ge(pairs_lo_made, LAST)
            sp.wait_ge(scratch_written, 16 * STRIPS * (LAST + TILES))
            for k, parts, src in pair_loads:
                sp.dma_start(pairs[parts, k, :], src).then_inc(last_pairs_loaded[k], 16)
            store_y(LAST - 1)
            store_y(LAST)
            sp.wait_ge(y_stored, 16 * MACROS)

        @block.gpsimd
        def _(pool):
            pool.memset(ident[:, :], 0.0).then_inc(ident_zero, 1)
            pool.iota(row_id[:, :], [[1, CHUNKS]], 0, CHUNKS).then_inc(row_ids_made, 1)
            pool.wait_ge(ident_zero, 1)
            pool.affine_select(out=ident[:, :], in_=ident[:, :], compare_op=ALU.not_equal, fill=1.0,
                               base=0, pattern=[[-1, P]], channel_multiplier=1).then_inc(ident_made, 1)

            def gather_tile(m, t, first):
                pool.wait_ge(idx_loaded[t], 16 * m + 16)
                if not first:
                    pool.wait_ge(transposed, 2 * NTR * (m - 1) + NTR * (t + 1))
                pool.sem_inc(tiles_begun, 1)
                for n, f in enumerate(GATHER_TABLES):
                    group = (1 + n) // 4
                    pool.indirect_dma_start(
                        out=rows[t][:, 1 + n, :], out_offset=None, in_=tables[f],
                        in_offset=bass.IndirectOffsetOnAxis(ap=idx[t][:, n:n + 1], axis=0),
                    ).then_inc(gathered[t][group], 16)

            for t in range(TILES):
                gather_tile(0, t, True)
            with pool.Fori(1, MACROS) as m:
                for t in range(TILES):
                    gather_tile(m, t, False)

        @block.tensor
        def _(pe):
            def transpose_group(m, t, g, first):
                f0, nf = TR_GROUPS[g]
                if g == 0:
                    pe.wait_ge(dense_loaded[t], 16 * m + 16)
                pe.wait_ge(gathered[t][g], 16 * GATHERS[g] * m + 16 * GATHERS[g])
                if g % 2 == 0:
                    n = TR_ACT * t + g // 2
                    if not (first and n == 0):
                        pe.wait_ge(tr_copied_act, 2 * TR_ACT * m + n)
                else:
                    n = TR_DVE * t + g // 2
                    if not (first and n == 0):
                        pe.wait_ge(tr_copied_dve, 2 * TR_DVE * m + n)
                for k in range(nf):
                    last = pe.transpose(TR[g % 2][:, k * P:(k + 1) * P], rows[t][:, f0 + k, :], ident[:, :])
                last.then_inc(transposed, 1)

            def lookup(m, n, first):
                b = n % 2
                pe.wait_ge(onehot_made, NO * m + n + 1)
                if not (first and n < 2):
                    pe.wait_ge(lookup_copied, NO * m + n - 1)
                if first:
                    pe.wait_ge(hi_made, n + 1)
                    pe.wait_ge(lo_made, n + 1)
                for q in range(CHUNKS):
                    at = slice(n * TABLE + q * D, n * TABLE + (q + 1) * D)
                    pe.matmul(OH[b][:, 0:MC], tab_hi[0:VROWS, at], onehot[n % ONEHOTS][0:VROWS, q, :],
                              start=(q == 0), stop=False)
                    last = pe.matmul(OH[b][:, 0:MC], tab_lo[0:VROWS, at], onehot[n % ONEHOTS][0:VROWS, q, :],
                                     start=False, stop=(q == CHUNKS - 1))
                last.then_inc(looked_up, 1)

            def gram_half(m, t, b, half, first):
                if half == 0:
                    if not (first and t == 0):
                        pe.wait_ge(gram_copied, 4 * m + 2 * t + b - 1)
                    if t == 0 and b == 0:
                        pe.wait_ge(lookup_copied, NO * m + NO)
                    if b == 0:
                        pe.wait_ge(tr_copied_act, 2 * TR_ACT * m + TR_ACT * (t + 1))
                        pe.wait_ge(tr_copied_dve, 2 * TR_DVE * m + TR_DVE * (t + 1))
                    if first and t == 0 and b == 0:
                        pe.wait_ge(gram_cleared, 2)
                hs = BANK_SAMPLES // 2
                for s in range(half * hs, (half + 1) * hs):
                    for g in range(STRIPS):
                        c = (g * TILES + t) * SS + b * BANK_SAMPLES + s
                        last = pe.matmul(GR[b][32 * g:32 * g + N, s * NCOL:(s + 1) * NCOL], ET[:, c, :], ET[:, c, 0:NCOL],
                                         start=True, stop=True)
                if half == 1:
                    last.then_inc(gram_done, 1)

            def split_product(out, w_hi, w_lo, x_hi, x_lo, start, stop):
                pe.matmul(out, w_hi, x_hi, start=start, stop=False)
                pe.matmul(out, w_hi, x_lo, start=False, stop=False)
                return pe.matmul(out, w_lo, x_hi, start=False, stop=stop)

            def layer1(u, c, first):
                if c == 0:
                    pe.wait_ge(pairs_lo_made, u + 1)
                    pe.wait_ge(denseT_lo_made, u + 1)
                    if first:
                        pe.wait_ge(hi_made, NJOBS)
                        pe.wait_ge(lo_made, NJOBS)
                    else:
                        pe.wait_ge(y_copied, u)
                elif c == 1:
                    if not first:
                        pe.wait_ge(h2_made, M2 * u)
                else:
                    pe.wait_ge(h1_hi_made, M1 * u + c - 1)
                out_c = ML[c % 2][:, 0:MC]
                split_product(out_c, wd_hi[:, c * P:(c + 1) * P], wd_lo[:, c * P:(c + 1) * P],
                              denseT_hi[:, :], denseT_lo[:, :], True, False)
                for k in range(NPCH):
                    at = slice(k * H1 + c * P, k * H1 + (c + 1) * P)
                    last = split_product(out_c, wp_hi[0:PCH, at], wp_lo[0:PCH, at],
                                         pairs_hi[0:PCH, k, :], pairs_lo[0:PCH, k, :], False, k == NPCH - 1)
                last.then_inc(l1_done, 1)

            def layer2(u, c):
                if c == 0:
                    pe.wait_ge(h1_hi_made, M1 * u + M1 - 1)
                for k in range(M1):
                    if c == 0:
                        pe.wait_ge(h1_lo_made, M1 * u + k + 1)
                    at = slice(k * H2 + c * P, k * H2 + (c + 1) * P)
                    last = split_product(ML[c % 2][:, 0:MC], w2_hi[:, at], w2_lo[:, at],
                                         h1_hi[:, k, :], h1_lo[:, k, :], k == 0, k == M1 - 1)
                last.then_inc(l2_done, 1)

            def last_layers():
                pe.wait_ge(denseT_lo_made, LAST + 1)
                pe.wait_ge(y_copied, LAST)
                pe.wait_ge(h2_made, M2 * LAST)
                pe.wait_ge(gram_copied, 4 * LAST + 4)
                for c in range(M1):
                    split_product(LAST_L1[c][:, 0:MC], wd_hi[:, c * P:(c + 1) * P], wd_lo[:, c * P:(c + 1) * P],
                                  denseT_hi[:, :], denseT_lo[:, :], True, False)
                for k in range(NPCH):
                    pe.wait_ge(pairs_lo_made, LAST + k + 1)
                    for c in range(M1):
                        at = slice(k * H1 + c * P, k * H1 + (c + 1) * P)
                        last = split_product(LAST_L1[c][:, 0:MC], wp_hi[0:PCH, at], wp_lo[0:PCH, at],
                                             pairs_hi[0:PCH, k, :], pairs_lo[0:PCH, k, :], False, k == NPCH - 1)
                        if k == NPCH - 1:
                            last.then_inc(l1_done, 1)
                for k in range(M1):
                    pe.wait_ge(h1_lo_made, M1 * LAST + k + 1)
                    for c in range(M2):
                        at = slice(k * H2 + c * P, k * H2 + (c + 1) * P)
                        last = split_product(LAST_L2[c][:, 0:MC], w2_hi[:, at], w2_lo[:, at],
                                             h1_hi[:, k, :], h1_lo[:, k, :], k == 0, k == M1 - 1)
                        if k == M1 - 1:
                            last.then_inc(l2_done, 1)
                layer3(LAST, False)

            def layer3(u, first):
                if first:
                    pe.wait_ge(weights_loaded, 16 * 3)
                pe.wait_ge(h2_made, M2 * u + M2)
                for a in range(MC // P):
                    for k in range(M2):
                        last = pe.matmul(ML[0][:, a:a + 1], h2[:, k, a * P:(a + 1) * P], w3s[:, k:k + 1],
                                         start=(k == 0), stop=(k == M2 - 1))
                last.then_inc(y_done, 1)

            def gram_bank(m, t, b, first):
                for half in range(2):
                    gram_half(m, t, b, half, first)

            def lookups_and_tile0(m, first, mlp):
                for n in range(NO - 2):
                    lookup(m, n, first)
                if first:
                    pe.wait_ge(ident_made, 1)
                transpose_group(m, 0, 0, first)
                transpose_group(m, 0, 1, first)
                lookup(m, NO - 2, first)
                transpose_group(m, 0, 2, first)
                transpose_group(m, 0, 3, first)
                lookup(m, NO - 1, first)
                for g in range(4, NTR):
                    transpose_group(m, 0, g, first)
                if mlp:
                    layer1(m - 1, 0, mlp == "first")
                    layer1(m - 1, 1, mlp == "first")
                gram_bank(m, 0, 0, first)
                if mlp:
                    layer1(m - 1, 2, mlp == "first")
                    layer1(m - 1, 3, mlp == "first")

            def tile1(m, first, mlp):
                gram_half(m, 0, 1, 0, first)
                transpose_group(m, 1, 0, first)
                transpose_group(m, 1, 1, first)
                gram_half(m, 0, 1, 1, first)
                transpose_group(m, 1, 2, first)
                transpose_group(m, 1, 3, first)
                if mlp:
                    layer2(m - 1, 0)
                for g in range(4, NTR):
                    transpose_group(m, 1, g, first)
                gram_bank(m, 1, 0, first)
                if mlp:
                    layer2(m - 1, 1)
                gram_bank(m, 1, 1, first)
                if mlp:
                    layer3(m - 1, mlp == "first")

            lookups_and_tile0(0, True, None)
            tile1(0, True, None)
            lookups_and_tile0(1, False, "first")
            tile1(1, False, "first")
            with pe.Fori(2, LAST) as m:
                lookups_and_tile0(m, False, "later")
                tile1(m, False, "later")

            lookups_and_tile0(LAST, False, "later")
            tile1(LAST, False, "later")
            for n in range(WARM):
                pe.matmul(OH[0][:, 0:MC], tab_hi[0:VROWS, 0:P], onehot[0][0:VROWS, 0, :], start=True, stop=True)
            last_layers()

        def et_tile(t, f0, nf):
            return ET[:, :, f0:f0 + nf].rearrange("p (g u s) f -> p u f g s", g=STRIPS, u=TILES)[:, t]

        def copy_group(copy, t, g):
            f0, nf = TR_GROUPS[g]
            return copy(et_tile(t, DENSE_SLOT + f0, nf),
                        TR[g % 2][:, 0:nf * P].rearrange("p (f g s) -> p f g s", g=STRIPS, s=SS))

        @block.scalar
        def _(act):
            def copy_lookup(m, n):
                act.wait_ge(looked_up, NO * m + n + 1)
                act.copy(ET[:, :, n], OH[n % 2][:, 0:MC]).then_inc(lookup_copied, 1)

            def copy_transposed(m, t, g, first=False):
                if t == 0 and g == 0 and not first:
                    act.wait_ge(denseT_lo_made, m)
                act.wait_ge(transposed, 2 * NTR * m + NTR * t + g + 1)
                copy_group(act.copy, t, g).then_inc(tr_copied_act, 1)

            def make_pairs_hi(m):
                act.wait_ge(pairs_loaded, 16 * LOADS * m + 16 * LOADS)
                act.copy(pairs_hi[0:PCH, :, :], pairs[0:PCH, :, :]).then_inc(pairs_hi_made, 1)

            def make_h1(u, c, first, src):
                act.wait_ge(l1_done, M1 * u + c + 1)
                if not (first and c < 2):
                    act.wait_ge(h1_lo_made, M1 * u + c - 1)
                if first and c == 0:
                    act.wait_ge(weights_loaded, 16 * 3)
                act.activation(h1f[c % 2], src[:, 0:MC], ACT.Relu, bias=b1s[:, c:c + 1])
                act.activation(h1_hi[:, c, :], src[:, 0:MC], ACT.Relu, bias=b1s[:, c:c + 1]) \
                   .then_inc(h1_hi_made, 1)

            def copy_gram(m, t, b, first):
                act.wait_ge(gram_done, 4 * m + 2 * t + b + 1)
                if t == 0 and b == 0:
                    if first:
                        act.wait_ge(hi_made, NO)
                        act.wait_ge(lo_made, NO)
                    else:
                        act.wait_ge(scratch_written, 16 * STRIPS * m)
                s0 = t * SS + b * BANK_SAMPLES
                act.copy(gram[:, :, s0:s0 + BANK_SAMPLES],
                         GR[b][:, 0:BANK_SAMPLES * NCOL].rearrange("p (s j) -> p j s", j=NCOL)).then_inc(gram_copied, 1)

            def make_h2(u, c, src):
                act.wait_ge(l2_done, M2 * u + c + 1)
                act.activation(h2[:, c, :], src[:, 0:MC], ACT.Relu, bias=b2s[:, c:c + 1]).then_inc(h2_made, 1)

            def copy_y(u, first):
                act.wait_ge(y_done, u + 1)
                if not first:
                    act.wait_ge(y_stored, 16 * u)
                act.copy(y[:, :], ML[0][:, 0:MC // P]).then_inc(y_copied, 1)

            def make_denseT_hi(m):
                act.wait_ge(tr_copied_act, 2 * TR_ACT * m + TR_ACT + 1)
                act.copy(denseT_hi[:, :], ET[:, :, DENSE_SLOT]).then_inc(denseT_hi_made, 1)

            def split_hi(n):
                _, parts, width, hi, _ = jobs[n]
                if n == NJOBS - 1:
                    act.wait_ge(wd_summed, 1)
                    width = H1
                else:
                    act.wait_ge(staged[buf[n]], 16 * use[n])
                act.copy(hi, stage[buf[n]][0:parts, 0:width]).then_inc(hi_made, 1)

            def lookups_and_tile0(m, first, mlp):
                for n in range(NO - 2):
                    if first and n + 2 < NO:
                        split_hi(n + 2)
                    copy_lookup(m, n)
                copy_transposed(m, 0, 0, first)
                if mlp:
                    make_pairs_hi(m - 1)
                copy_lookup(m, NO - 2)
                copy_transposed(m, 0, 2)
                copy_lookup(m, NO - 1)
                for g in range(4, NTR, 2):
                    copy_transposed(m, 0, g)
                if mlp:
                    make_h1(m - 1, 0, mlp == "first", ML[0])
                    make_h1(m - 1, 1, mlp == "first", ML[1])
                copy_gram(m, 0, 0, first)
                if mlp:
                    make_h1(m - 1, 2, mlp == "first", ML[0])
                    make_h1(m - 1, 3, mlp == "first", ML[1])

            def tile1(m, first, mlp):
                copy_transposed(m, 1, 0)
                copy_gram(m, 0, 1, first)
                if first:
                    split_hi(NO)
                copy_transposed(m, 1, 2)
                if mlp:
                    make_h2(m - 1, 0, ML[0])
                for g in range(4, NTR, 2):
                    copy_transposed(m, 1, g)
                make_denseT_hi(m)
                if first:
                    split_hi(NO + 1)
                copy_gram(m, 1, 0, first)
                if first:
                    split_hi(NO + 2)
                if mlp:
                    make_h2(m - 1, 1, ML[1])
                copy_gram(m, 1, 1, first)
                if first:
                    split_hi(NO + 3)
                if mlp:
                    copy_y(m - 1, mlp == "first")

            split_hi(0)
            split_hi(1)
            lookups_and_tile0(0, True, None)
            tile1(0, True, None)
            lookups_and_tile0(1, False, "first")
            tile1(1, False, "first")
            with act.Fori(2, LAST) as m:
                lookups_and_tile0(m, False, "later")
                tile1(m, False, "later")

            lookups_and_tile0(LAST, False, "later")
            tile1(LAST, False, "later")
            for k in range(NPCH):
                act.wait_ge(last_pairs_loaded[k], 16 * [chunk for chunk, _, _ in pair_loads].count(k))
                act.copy(pairs_hi[0:PCH, k, :], pairs[0:PCH, k, :]).then_inc(pairs_hi_made, 1)
            for c in range(M1):
                make_h1(LAST, c, False, LAST_L1[c])
            for c in range(M2):
                make_h2(LAST, c, LAST_L2[c])
            copy_y(LAST, False)

        @block.vector
        def _(dve):
            def make_onehot(m, n, first):
                if first and n == 0:
                    dve.wait_ge(first_ids_loaded, 16)
                if n == (2 if first else 0):
                    dve.wait_ge(ids_loaded, 16 * m + 16)
                if not (first and n < ONEHOTS):
                    dve.wait_ge(looked_up, NO * m + n - ONEHOTS + 1)
                dve.tensor_tensor(
                    onehot[n % ONEHOTS][0:VROWS, :, :],
                    ids_b[0:VROWS, n, :].unsqueeze(1).to_broadcast([VROWS, CHUNKS, MC]),
                    row_id[0:VROWS, :].unsqueeze(2).to_broadcast([VROWS, CHUNKS, MC]),
                    ALU.is_equal).then_inc(onehot_made, 1)

            def copy_transposed(m, t, g):
                dve.wait_ge(transposed, 2 * NTR * m + NTR * t + g + 1)
                copy_group(dve.tensor_copy, t, g).then_inc(tr_copied_dve, 1)

            def make_pairs_lo(m):
                dve.wait_ge(pairs_hi_made, m + 1)
                dve.tensor_tensor(pairs_lo[0:PCH, :, :], pairs[0:PCH, :, :], pairs_hi[0:PCH, :, :].bitcast(F32),
                                  ALU.subtract).then_inc(pairs_lo_made, 1)

            def make_denseT_lo(m):
                dve.wait_ge(denseT_hi_made, m + 1)
                dve.tensor_tensor(denseT_lo[:, :], ET[:, :, DENSE_SLOT], denseT_hi[:, :].bitcast(F32),
                                  ALU.subtract).then_inc(denseT_lo_made, 1)

            def make_h1_lo(u, c):
                dve.wait_ge(h1_hi_made, M1 * u + c + 1)
                dve.tensor_tensor(h1_lo[:, c, :], h1f[c % 2], h1_hi[:, c, :].bitcast(F32),
                                  ALU.subtract).then_inc(h1_lo_made, 1)

            def split_lo(n):
                _, parts, width, hi, lo = jobs[n]
                if n == NJOBS - 1:
                    dve.wait_ge(staged[buf[n]], 16 * use[n])
                    width = H1
                    st = stage[buf[n]]
                    dve.tensor_tensor(st[:, 0:H1], st[:, 0:H1], st[:, H1:2 * H1], ALU.add).then_inc(wd_summed, 1)
                dve.wait_ge(hi_made, n + 1)
                dve.tensor_tensor(lo, stage[buf[n]][0:parts, 0:width], hi.bitcast(F32),
                                  ALU.subtract).then_inc(lo_made, 1)

            for b in range(2):
                dve.memset(GR[b][:, :], 0.0).then_inc(gram_cleared, 1)
            dve.wait_ge(row_ids_made, 1)
            make_onehot(0, 0, True)
            make_onehot(0, 1, True)
            for n in range(NO):
                split_lo(n)
                if n >= 2:
                    make_onehot(0, n, True)
                if n == NO - 2:
                    copy_transposed(0, 0, 1)
            copy_transposed(0, 0, 3)
            copy_transposed(0, 1, 1)
            split_lo(NO)
            copy_transposed(0, 1, 3)
            make_onehot(1, 0, False)
            make_denseT_lo(0)
            split_lo(NO + 1)
            make_onehot(1, 1, False)
            split_lo(NO + 2)
            make_onehot(1, 2, False)
            split_lo(NO + 3)
            make_onehot(1, 3, False)

            def macro(m, last):
                for n in range(ONEHOTS, NO):
                    make_onehot(m, n, False)
                copy_transposed(m, 0, 1)
                make_pairs_lo(m - 1)
                copy_transposed(m, 0, 3)
                make_h1_lo(m - 1, 0)
                make_h1_lo(m - 1, 1)
                if not last:
                    make_onehot(m + 1, 0, False)
                make_h1_lo(m - 1, 2)
                make_h1_lo(m - 1, 3)
                copy_transposed(m, 1, 1)
                if not last:
                    make_onehot(m + 1, 1, False)
                copy_transposed(m, 1, 3)
                make_denseT_lo(m)
                if not last:
                    for n in range(2, ONEHOTS):
                        make_onehot(m + 1, n, False)

            with dve.Fori(1, LAST) as m:
                macro(m, False)

            macro(LAST, True)
            for k in range(NPCH):
                dve.wait_ge(pairs_hi_made, LAST + k + 1)
                dve.tensor_tensor(pairs_lo[0:PCH, k, :], pairs[0:PCH, k, :], pairs_hi[0:PCH, k, :].bitcast(F32),
                                  ALU.subtract).then_inc(pairs_lo_made, 1)
            for c in range(M1):
                make_h1_lo(LAST, c)


def _pair_rows():
    found = []
    for i in range(N):
        for k in range(1, NK + 1):
            slots = divmod(i * N + k, NCOL) if i < N - 1 else (i, NK - 1 + k)
            a, b = sorted(SLOT_FEATURE[slot] for slot in slots)
            found.append(D + a * N - a * (a + 1) // 2 + b - a - 1)
    return np.array(found)


def kernel(**inputs):
    import concourse.bacc as bacc
    from concourse.bass_utils import run_bass_kernel_spmd

    def tiled(a):
        a = a.reshape(MACROS, STRIPS, TILES, SS, a.shape[1]).transpose(0, 2, 1, 3, 4)
        return a.reshape(MACROS * TILES, P, a.shape[-1])

    ids = np.asarray(inputs["ids"])
    w_top1 = np.asarray(inputs["W_top1"])
    ends = w_top1.shape[0] - D
    arrays = {
        "dense": tiled(np.asarray(inputs["r_dense_features"])),
        "ids_gather": tiled(ids[:, GATHER_TABLES]),
        "ids_onehot": ids[:, ONEHOT_TABLES].reshape(MACROS, MC, NO).transpose(0, 2, 1),
        "w_dense": np.stack([w_top1[0:D], w_top1[ends:ends + D]], axis=1),
        "w_pairs": w_top1[_pair_rows()].reshape(NPCH, PCH, H1).transpose(1, 0, 2),
        "b1": np.asarray(inputs["b_top1"]).reshape(M1, P).T,
        "w2": np.asarray(inputs["W_top2"]).reshape(M1, P, H2).transpose(1, 0, 2),
        "b2": np.asarray(inputs["b_top2"]).reshape(M2, P).T,
        "w3": np.asarray(inputs["W_top3"]).reshape(M2, P).T,
    }
    for f in range(FIELDS):
        arrays[f"tbl_{f}"] = np.asarray(inputs[f"tbl_{f}"])
    arrays = {name: np.ascontiguousarray(a) for name, a in arrays.items()}

    nc = bacc.Bacc("TRN2", target_bir_lowering=False, num_devices=1)
    aps = {name: nc.dram_tensor(name, a.shape, mybir.dt.from_np(a.dtype), kind="ExternalInput").ap()
           for name, a in arrays.items()}
    out = nc.dram_tensor("out", (MACROS, P, MC // P), mybir.dt.float32, kind="ExternalOutput").ap()
    build(nc, aps["dense"], aps["ids_gather"], aps["ids_onehot"], [aps[f"tbl_{f}"] for f in range(FIELDS)],
          aps["w_dense"], aps["w_pairs"], aps["b1"], aps["w2"], aps["b2"], aps["w3"], out)
    r = run_bass_kernel_spmd(nc, [arrays], core_ids=[0])
    y = r.results[0]["out"].reshape(MACROS, P, MC // P)
    return y.transpose(0, 2, 1).reshape(BATCH, 1)
```
